# Optimizing a Trainium2 kernel written in Bass

```python
import numpy as np
import jax
import jax.numpy as jnp

def _softmax(x, axis=-1):
    return jax.nn.softmax(x, axis=axis)

def _gelu(x):
    return jax.nn.gelu(x, approximate=True)

def _silu(x):
    return jax.nn.silu(x)

def _sigmoid(x):
    return jax.nn.sigmoid(x)

def _layernorm(x, axis=-1, eps=1e-05):
    m = jnp.mean(x, axis=axis, keepdims=True)
    v = jnp.var(x, axis=axis, keepdims=True)
    return (x - m) / jnp.sqrt(v + eps)

def _scatter_add(tgt, idx, src, axis=0):
    return tgt.at[idx].add(src)

def _segment_sum(src, seg, n):
    return jax.ops.segment_sum(src, seg, n)
kernel_name = 'mk_adj_preln_d2_adj_r2_a16054'

def setup_inputs(seed: int=0):
    np.random.seed(seed)
    _w = jnp.asarray

    def _rec_inputs():
        import jax
        import jax.numpy as jnp
        _gk = jax.random.key(seed)
        x = -0.0001538 + 1 * jax.random.normal(jax.random.fold_in(_gk, 1), (128, 64, 384), jnp.float32)
        _a = jax.random.bernoulli(jax.random.fold_in(_gk, 2), 0.125, (128, 64, 64))
        _a = jnp.logical_or(_a, jnp.swapaxes(_a, -1, -2))
        _a = jnp.logical_or(_a, jnp.eye(64, dtype=bool))
        _af = _a.astype(jnp.float32)
        _af = _af * jax.random.uniform(jax.random.fold_in(_gk, 3), (128, 64, 64), jnp.float32, 0.05, 0.999992)
        adj = _af
        return (x, adj)
    x, adj = _rec_inputs()

    def _L0_gnn_setup():
        import jax, jax.numpy as jnp
        import numpy as np
        B, N, D, H = (8, 512, 384, 12)
        HD = D // H

        def _split_heads(x):
            b, n, _ = x.shape
            return x.reshape(b, n, H, HD).transpose(0, 2, 1, 3)
        key = jax.random.key(seed)
        ks = jax.random.split(key, 10)
        input_graph = jax.random.normal(ks[0], (B, N, D), dtype=jnp.float32)
        u = jax.random.uniform(ks[1], (B, N, N), dtype=jnp.float32)
        keep = jax.random.uniform(ks[2], (B, N, N)) < 0.15
        adj = jnp.where(keep, u, 0.0)
        s = 1.0 / np.sqrt(D)
        Wq = jax.random.normal(ks[3], (D, D), dtype=jnp.float32) * s
        bq = jnp.zeros((D,), dtype=jnp.float32)
        Wk = jax.random.normal(ks[4], (D, D), dtype=jnp.float32) * s
        bk = jnp.zeros((D,), dtype=jnp.float32)
        Wv = jax.random.normal(ks[5], (D, D), dtype=jnp.float32) * s
        bv = jnp.zeros((D,), dtype=jnp.float32)
        beta = jnp.asarray(0.1, dtype=jnp.float32)
        return {'input_graph': input_graph, 'adj': adj, 'Wq': Wq, 'bq': bq, 'Wk': Wk, 'bk': bk, 'Wv': Wv, 'bv': bv, 'beta': beta}
    _L0_gnn_all = _L0_gnn_setup()
    _L0_gnn_in = {k: v for k, v in _L0_gnn_all.items() if k in ('Wq', 'bq', 'Wk', 'bk', 'Wv', 'bv', 'beta')}
    del _L0_gnn_all

    def _L1_gnn_setup():
        import jax, jax.numpy as jnp
        import numpy as np
        LN_EPS = 1e-12

        def _digcn_forward(hidden_state, adjacency_matrix, Wl, bl, Ws, bs, Wr, br, ln_w, ln_b):
            B, S, D = hidden_state.shape
            temper = jnp.asarray(D, jnp.float32) ** 0.5
            i = jnp.arange(S)
            upper = (i[None, :] > i[:, None]).astype(hidden_state.dtype)
            lower = (i[None, :] < i[:, None]).astype(hidden_state.dtype)

            def layer(h, params):
                wl, b_l, ws, b_s, wr, b_r, g, beta = params
                u = jnp.einsum('bid,bjd->bij', h, h) / temper
                a = jax.nn.softmax(u, axis=-1)
                delta = a * adjacency_matrix
                attn = delta / (jnp.sum(delta, axis=-1, keepdims=True) + 1e-10)
                hl = h @ wl.T + b_l
                hs = h @ ws.T + b_s
                hr = h @ wr.T + b_r
                diag_a = jnp.diagonal(attn, axis1=1, axis2=2)
                ctx = jnp.einsum('bij,bjd->bid', attn * upper, hl) + diag_a[..., None] * hs + jnp.einsum('bij,bjd->bid', attn * lower, hr)
                mean = ctx.mean(-1, keepdims=True)
                var = ctx.var(-1, keepdims=True)
                o = (ctx - mean) / jnp.sqrt(var + LN_EPS) * g + beta
                return (jax.nn.relu(o), None)
            out, _ = jax.lax.scan(layer, hidden_state, (Wl, bl, Ws, bs, Wr, br, ln_w, ln_b))
            return out
        key = jax.random.key(seed)
        ks = jax.random.split(key, 6)
        B, S, D, L = (8, 512, 384, 2)
        scale = (1.0 / D) ** 0.5
        hidden_state = jax.random.normal(ks[0], (B, S, D), jnp.float32)
        adjacency_matrix = (jax.random.uniform(ks[1], (B, S, S)) < 0.05).astype(jnp.float32)
        Wl = jax.random.normal(ks[2], (L, D, D), jnp.float32) * scale
        Ws = jax.random.normal(ks[3], (L, D, D), jnp.float32) * scale
        Wr = jax.random.normal(ks[4], (L, D, D), jnp.float32) * scale
        bl = jnp.zeros((L, D), jnp.float32)
        bs = jnp.zeros((L, D), jnp.float32)
        br = jnp.zeros((L, D), jnp.float32)
        ln_w = jnp.ones((L, D), jnp.float32)
        ln_b = jnp.zeros((L, D), jnp.float32)
        return dict(hidden_state=hidden_state, adjacency_matrix=adjacency_matrix, Wl=Wl, bl=bl, Ws=Ws, bs=bs, Wr=Wr, br=br, ln_w=ln_w, ln_b=ln_b)
    _L1_gnn_all = _L1_gnn_setup()
    _L1_gnn_in = {k: v for k, v in _L1_gnn_all.items() if k in ('Wl', 'bl', 'Ws', 'bs', 'Wr', 'br', 'ln_w', 'ln_b')}
    del _L1_gnn_all
    return {'x': x, 'adj': adj, 'L0_gnn_Wq': _L0_gnn_in['Wq'], 'L0_gnn_bq': _L0_gnn_in['bq'], 'L0_gnn_Wk': _L0_gnn_in['Wk'], 'L0_gnn_bk': _L0_gnn_in['bk'], 'L0_gnn_Wv': _L0_gnn_in['Wv'], 'L0_gnn_bv': _L0_gnn_in['bv'], 'L0_gnn_beta': _L0_gnn_in['beta'], 'L1_gnn_Wl': _L1_gnn_in['Wl'], 'L1_gnn_bl': _L1_gnn_in['bl'], 'L1_gnn_Ws': _L1_gnn_in['Ws'], 'L1_gnn_bs': _L1_gnn_in['bs'], 'L1_gnn_Wr': _L1_gnn_in['Wr'], 'L1_gnn_br': _L1_gnn_in['br'], 'L1_gnn_ln_w': _L1_gnn_in['ln_w'], 'L1_gnn_ln_b': _L1_gnn_in['ln_b']}

def reference(x, adj, L0_gnn_Wq, L0_gnn_bq, L0_gnn_Wk, L0_gnn_bk, L0_gnn_Wv, L0_gnn_bv, L0_gnn_beta, L1_gnn_Wl, L1_gnn_bl, L1_gnn_Ws, L1_gnn_bs, L1_gnn_Wr, L1_gnn_br, L1_gnn_ln_w, L1_gnn_ln_b):
    import jax
    import jax.numpy as jnp

    def _L0_gnn_ref(input_graph, adj, Wq, bq, Wk, bk, Wv, bv, beta):
        import jax, jax.numpy as jnp
        import numpy as np
        B, N, D, H = (8, 512, 384, 12)
        HD = D // H

        def _split_heads(x):
            b, n, _ = x.shape
            return x.reshape(b, n, H, HD).transpose(0, 2, 1, 3)
        q = _split_heads(input_graph @ Wq + bq)
        k = _split_heads(input_graph @ Wk + bk)
        v = _split_heads(input_graph @ Wv + bv)
        scores = jnp.einsum('bhqd,bhkd->bhqk', q, k) / jnp.sqrt(jnp.asarray(HD, input_graph.dtype))
        adj_e = adj[:, None, :, :]
        scores = scores + beta * adj_e
        scores = jnp.where(adj_e > 0, scores, jnp.asarray(-9000000000000000.0, scores.dtype))
        probs = jax.nn.softmax(scores, axis=-1)
        out = jnp.einsum('bhqk,bhkd->bhqd', probs, v)
        return out.transpose(0, 2, 1, 3).reshape(input_graph.shape[0], input_graph.shape[1], D)

    def _L1_gnn_ref(hidden_state, adjacency_matrix, Wl, bl, Ws, bs, Wr, br, ln_w, ln_b):
        import jax, jax.numpy as jnp
        import numpy as np
        LN_EPS = 1e-12

        def _digcn_forward(hidden_state, adjacency_matrix, Wl, bl, Ws, bs, Wr, br, ln_w, ln_b):
            B, S, D = hidden_state.shape
            temper = jnp.asarray(D, jnp.float32) ** 0.5
            i = jnp.arange(S)
            upper = (i[None, :] > i[:, None]).astype(hidden_state.dtype)
            lower = (i[None, :] < i[:, None]).astype(hidden_state.dtype)

            def layer(h, params):
                wl, b_l, ws, b_s, wr, b_r, g, beta = params
                u = jnp.einsum('bid,bjd->bij', h, h) / temper
                a = jax.nn.softmax(u, axis=-1)
                delta = a * adjacency_matrix
                attn = delta / (jnp.sum(delta, axis=-1, keepdims=True) + 1e-10)
                hl = h @ wl.T + b_l
                hs = h @ ws.T + b_s
                hr = h @ wr.T + b_r
                diag_a = jnp.diagonal(attn, axis1=1, axis2=2)
                ctx = jnp.einsum('bij,bjd->bid', attn * upper, hl) + diag_a[..., None] * hs + jnp.einsum('bij,bjd->bid', attn * lower, hr)
                mean = ctx.mean(-1, keepdims=True)
                var = ctx.var(-1, keepdims=True)
                o = (ctx - mean) / jnp.sqrt(var + LN_EPS) * g + beta
                return (jax.nn.relu(o), None)
            out, _ = jax.lax.scan(layer, hidden_state, (Wl, bl, Ws, bs, Wr, br, ln_w, ln_b))
            return out
        return _digcn_forward(hidden_state, adjacency_matrix, Wl, bl, Ws, bs, Wr, br, ln_w, ln_b)
    h = jnp.maximum(_layernorm(x, axis=-1), 0.0)
    x = x + _L0_gnn_ref(h, adj, L0_gnn_Wq, L0_gnn_bq, L0_gnn_Wk, L0_gnn_bk, L0_gnn_Wv, L0_gnn_bv, L0_gnn_beta)
    h = jnp.maximum(_layernorm(x, axis=-1), 0.0)
    x = x + _L1_gnn_ref(h, adj, L1_gnn_Wl, L1_gnn_bl, L1_gnn_Ws, L1_gnn_bs, L1_gnn_Wr, L1_gnn_br, L1_gnn_ln_w, L1_gnn_ln_b)
    return x

_drawn_inputs = setup_inputs


def setup_inputs(seed=0):
    import zlib

    import numpy as np

    out = dict(_drawn_inputs(seed))
    spreads = {'L0_gnn_bq': (0.0, 0.8),
     'L0_gnn_bk': (0.0, 0.8),
     'L0_gnn_bv': (0.0, 0.1),
     'L1_gnn_bl': (0.0, 0.59),
     'L1_gnn_bs': (0.0, 0.1),
     'L1_gnn_br': (0.0, 0.53),
     'L1_gnn_ln_w': (1.0, 0.2),
     'L1_gnn_ln_b': (0.0, 0.1)}
    factors = {}
    for name, (base, spread) in spreads.items():
        noise = np.random.default_rng([zlib.crc32(name.encode()), seed]).standard_normal(out[name].shape)
        drawn = base * np.exp(spread * noise) if base else spread * noise
        out[name] = jnp.asarray(drawn.astype(out[name].dtype))
    for name, factor in factors.items():
        out[name] = (out[name] * factor).astype(out[name].dtype)
    return out
```

```python
from contextlib import ExitStack

import concourse.bass as bass
from concourse import mybir

ALU = mybir.AluOpType
ACT = mybir.ActivationFunctionType
F32 = mybir.dt.float32
F32R = mybir.dt.float32r
F16 = mybir.dt.float16
AX_X = mybir.AxisListType.X

P = 128
N = 64
G = P // N
T = 2
UN = T * P
UG = T * G
D = 384
C = D // P
H = 12
HD = D // H
HC = H // C
PAIRS = H // 2
BP = PAIRS // 2
VC = HD + 1
BANK = 512

LN_EPS = (1e-5, 1e-5, 1e-12, 1e-12)
MASKED = -9000000000000000.0

WQ, WK, WV = 0, 1, 2


def wround(r, which):
    return 3 + 3 * r + which


FILLS = (
    [("QK", k) for k in range(3)]
    + [("TF", 0), ("TF", 1), ("TE", 0), ("TE", 1), ("V", 0), ("V", 1), ("UF", 0), ("UE", 0)]
    + [("DF", k) for k in range(3)] + [("AF", 0)] + [("DF", k) for k in range(3, 6)]
    + [("S", k) for k in range(4)] + [("CF", 0), ("CF", 1)]
    + [("DE", k) for k in range(3)] + [("AE", 0)] + [("DE", k) for k in range(3, 6)]
    + [("P", k) for k in range(4)] + [("CE", 0), ("CE", 1), ("TA", 0), ("TA", 1), ("O", 0), ("O", 1)]
)
PER = {}
for _g, _k in FILLS:
    PER[_g] = PER.get(_g, 0) + 1
LAG = {"QK": 0, "V": 0, "S": 0, "P": 0, "O": 0, "TA": -1,
       "TE": 1, "UE": 1, "DE": 1, "AE": 1, "CE": 1,
       "TF": 2, "UF": 2, "DF": 2, "AF": 2, "CF": 2}


def banks():
    out, n = {}, 0
    for fill in FILLS:
        if fill[0] == "AF":
            out[fill] = (n + 4) % 8
        else:
            out[fill] = n % 8
            n += 1
    return out


BANK_OF = banks()

COUNTS = {
    "x_in": 16, "xres_in": 16, "adj0_in": 32, "adjE_in": 16, "adjF_in": 16,
    "qx_moved": 16 * 2 * HC, "x1_moved": 16, "stored": 16,
    "q_hi": 6, "tA_hi": 2, "tE_hi": 2, "tF_hi": 3, "tF_full": 3, "v_hi": 2,
    "u_hhE": 2, "u_hhF": 2, "expE": 1, "expF": 1, "d_hiE": 4, "d_hiF": 4, "hsE": 2, "hsF": 2,
    "a_hiE": 1, "a_hiF": 1, "exp0": 2, "p_hi": 8,
    "q_lo": 6, "tA_lo": 2, "tE_lo": 2, "v_lo": 2, "a_loE": 1, "a_loF": 1, "d_loE": 4, "d_loF": 4,
    "u_sumE": 2, "u_sumF": 2, "u_maxE": 1, "u_maxF": 1, "u_subE": 1, "u_subF": 1,
    "esumE": 1, "esumF": 1, "easumE": 1, "easumF": 1, "denE": 1, "denF": 1, "rdenE": 1, "rdenF": 1,
    "attnE": 1, "attnF": 1, "diagE": 1, "diagF": 1,
    "s_t": 1, "madd": 1, "s_sum": 4, "s_max": 2, "p_lo": 8, "osum": 2, "o_ready": 2,
    "c_readyE": 2, "c_readyF": 2, "zF": 2, "zE": 2, "z0": 2, "z1": 2, "out_ready": 2,
    "stats0": 2, "stats1": 2, "statsE": 2, "statsF": 2,
    "mv0": 2, "mv1": 2, "mvE": 2, "mvF": 2, "ve0": 1, "ve1": 1, "veE": 1, "veF": 1,
    "tF_lo": 1, "eaE": 1, "eaF": 1, "deE": 1, "deF": 1, "maskedE": 2, "maskedF": 2,
    "rstd0": 1, "rstd1": 1, "rstdE": 1, "rstdF": 1,
    "xb": 1, "s_sub": 2, "x1": 2, "yg": 2, "yb": 2,
}


def build(nc, x, adj, weights, cols, rows, biases, beta, out):
    U = x.shape[0] // UG
    ctx = ExitStack()
    with ctx:
        def sb(name, shape, dt=F32):
            return ctx.enter_context(nc.sbuf_tensor(name, shape, dt))

        w_hi = sb("w_hi", [P, 9, C, D], F32R)
        w_lo = sb("w_lo", [P, 9, C, D], F32R)
        param_cols = sb("param_cols", [P, 4, C])
        param_rows = sb("param_rows", [P, 3, D])
        beta_col = sb("beta_col", [P, 1])
        bias2 = sb("bias2", [2, 6, D], F32R)
        ones2 = sb("ones2", [2, P], F32R)
        ident = sb("ident", [P, P])
        eye = sb("eye", [P, N])
        later = sb("later", [P, P])
        earlier = sb("earlier", [P, P])
        half_power = sb("half_power", [P, T])
        x_ln = sb("x_ln", [P, T, D])
        x_res = sb("x_res", [P, T, D])
        adj0 = sb("adj0", [P, UG, N])
        madd = sb("madd", [P, UG, N])
        hT = {s: sb(f"hT_{s}", [P, C, 2, UN], F32R) for s in "AEF"}
        hT_full = sb("hT_full", [P, C, UN])
        q_half = [sb(f"q_{n}", [P, C, UN], F16) for n in ("hi", "lo")]
        k_half = [sb(f"k_{n}", [P, C, UN], F16) for n in ("hi", "lo")]
        qx = [sb(f"qx_{n}", [P, C * UG, HC, N], F16) for n in ("hi", "lo")]
        v_half = [sb(f"v_{n}", [P, T, H, VC], F16) for n in ("hi", "lo")]
        s = sb("s", [P, T, PAIRS, P])
        s_max = sb("s_max", [P, T, PAIRS * G])
        px = [sb(f"px_{n}", [P, T, H, G, N], F16) for n in ("hi", "lo")]
        o_rsum = sb("o_rsum", [P, T, H])
        o = hT_full[:, :, :].rearrange("p c n -> p (c n)").rearrange("p (t d) -> p t d", t=T)
        x1_new = sb("x1_new", [P, T, D])
        x1_old = sb("x1_old", [P, T, D])
        z1 = sb("z1", [P, T, D])
        adjs = {s_: sb(f"adj_{s_}", [P, T, N]) for s_ in "EF"}
        u_s = {s_: sb(f"u_{s_}", [P, T, N]) for s_ in "EF"}
        u_max = {s_: sb(f"u_max_{s_}", [P, T]) for s_ in "EF"}
        ea = {s_: sb(f"ea_{s_}", [P, T, N]) for s_ in "EF"}
        esum = {s_: sb(f"esum_{s_}", [P, T]) for s_ in "EF"}
        easum = {s_: sb(f"easum_{s_}", [P, T]) for s_ in "EF"}
        den = {s_: sb(f"den_{s_}", [P, T]) for s_ in "EF"}
        rden = {s_: sb(f"rden_{s_}", [P, T]) for s_ in "EF"}
        diag = {s_: sb(f"diag_{s_}", [P, T]) for s_ in "EF"}
        attn = {s_: sb(f"attn_{s_}", [P, T, G, N]) for s_ in "EF"}
        a_half = sb("a_half", [P, 2, T, P], F32R)
        a_masked = sb("a_masked", [P, 2, 2, T, P], F32R)
        d_half = sb("d_half", [P, T, 2, 2, D], F32R)
        hs = sb("hs", [P, T, D])
        c_s = {s_: sb(f"c_{s_}", [P, T, D]) for s_ in "EF"}
        stats = {s_: sb(f"stats_{s_}", [P, T, 6]) for s_ in "01EF"}
        mv = {s_: sb(f"mv_{s_}", [P, T, 2]) for s_ in "01EF"}
        ve = {s_: sb(f"ve_{s_}", [P, T]) for s_ in "01EF"}
        rstd = {s_: sb(f"rstd_{s_}", [P, T]) for s_ in "01EF"}
        w_stage = [b.rearrange("p (c n) -> p c n", c=C) for b in (
            s[:, :, :, :].rearrange("p t a b -> p (t a b)")[:, 0:C * D],
            px[0][:, :, :, :, :].rearrange("p t h g q -> p (t h g q)").bitcast(F32)[:, 0:C * D],
            qx[0][:, :, :, :].rearrange("p a b c -> p (a b c)").bitcast(F32)[:, 0:C * D])]
        bias_raw = [b.rearrange("p (a d) -> p a d", d=D) for b in (
            px[1][0:2, :, :, :, :].rearrange("p t h g q -> p (t h g q)").bitcast(F32)[:, 0:3 * D],
            qx[1][0:2, :, :, :].rearrange("p a b c -> p (a b c)").bitcast(F32)[:, 0:3 * D])]

        bank = [ctx.enter_context(nc.psum_tensor(f"bank{b}", [P, BANK], F32)) for b in range(8)]

        sem = {n: ctx.enter_context(nc.semaphore(n)) for n in COUNTS}
        filled = {g: ctx.enter_context(nc.semaphore(f"filled_{g}")) for g in PER}
        const_in = ctx.enter_context(nc.semaphore("const_in"))
        w_in = [ctx.enter_context(nc.semaphore(f"w_in{n}")) for n in range(3)]
        w_hi_done = ctx.enter_context(nc.semaphore("w_hi_done"))
        w_lo_done = ctx.enter_context(nc.semaphore("w_lo_done"))
        pool_const = ctx.enter_context(nc.semaphore("pool_const"))
        dve_const = ctx.enter_context(nc.semaphore("dve_const"))

        def live(u):
            return not isinstance(u, int) or 0 <= u < U

        def due(name, u, k=None):
            return u * COUNTS[name] + (COUNTS[name] if k is None else k)

        def wait(eng, name, u, k=None):
            if live(u):
                eng.wait_ge(sem[name], due(name, u, k))

        def wait_filled(eng, g, u, k):
            eng.wait_ge(filled[g], u * PER[g] + k + 1)

        def ps(g, k):
            return bank[BANK_OF[g, k]]

        def wait_bank(pe, i, g, k):
            at = FILLS.index((g, k))
            mine = BANK_OF[g, k]
            earlier_fills = [(f, 0) for f in reversed(FILLS[:at])]
            for back in (1, 2, 3):
                earlier_fills += [(f, back) for f in reversed(FILLS)]
            for (pg, pk), back in earlier_fills:
                u = i - back - LAG[pg]
                if BANK_OF[pg, pk] == mine and live(u):
                    wait(pe, *last_read(pg, pk, u))
                    return

        def last_read(g, k, u):
            name, at = {
                "QK": ("q_lo", 2 * k + 2), "V": ("v_lo", k + 1), "S": ("s_sum", k + 1),
                "P": ("p_lo", 2 * k + 2), "O": ("o_ready", k + 1), "TF": ("tF_hi", 2 + k),
                "T" + g[1:]: ("t" + g[1:] + "_lo", k + 1) if g != "TF" else ("tF_hi", 2 + k),
                "U" + g[1:]: ("u_sum" + g[1:], 2), "A" + g[1:]: ("a_lo" + g[1:], 1),
                "D" + g[1:]: ("hs" + g[1:], k // 3 + 1) if k % 3 == 1 else ("d_lo" + g[1:], 2 * (k // 3) + (k % 3) // 2 + 1),
                "C" + g[1:]: ("c_ready" + g[1:], k + 1),
            }[g]
            return name, u, at

        block = ctx.enter_context(nc.Block())

        SPECIAL_FIRST = range(-1, 3)
        LOOP = (3, U - 1)
        SPECIAL_LAST = range(U - 1, U + 2)

        def iterations(eng, body):
            for i in SPECIAL_FIRST:
                body(i)
            with eng.Fori(*LOOP) as i:
                body(i)
            for i in SPECIAL_LAST:
                body(i)

        @block.sync
        def _(sp):
            def x_rows(u):
                return x.rearrange("b n d -> (b n) d")[bass.ds(u * UN, UN), :].rearrange("(t p) d -> p t d", p=P)

            def adj_rows(u):
                return adj.rearrange("b i j -> (b i) j")[bass.ds(u * UN, UN), :].rearrange("(t p) j -> p t j", p=P)

            def load_adj0(u):
                src = adj[bass.ds(u * UG, UG), :, :].rearrange("g q k -> q g k")
                for h in range(2):
                    sp.dma_start(adj0[h * N:(h + 1) * N, :, :], src).then_inc(sem["adj0_in"], 16)

            sp.dma_start(x_ln[:, :, :], x_rows(0)).then_inc(sem["x_in"], 16)
            for n in range(9):
                if n >= 3:
                    sp.wait_ge(w_lo_done, n - 2)
                sp.dma_start(w_stage[n % 3], weights[n, :, :].rearrange("(c p) n -> p c n", p=P)).then_inc(w_in[n % 3], 16)
                if n == 0:
                    sp.dma_start(param_cols[:, :, :], cols).then_inc(const_in, 16)
                    sp.dma_start(param_rows[:, :, :].rearrange("p a d -> p (a d)"),
                                 rows.partition_broadcast(P)).then_inc(const_in, 16)
                    sp.dma_start(beta_col[:, :], beta.partition_broadcast(P)).then_inc(const_in, 16)
                    for r in range(2):
                        sp.dma_start(bias_raw[r], biases[r, :, :].partition_broadcast(2)).then_inc(const_in, 16)
            load_adj0(0)

            def body(i):
                if live(i + 1) and live(i):
                    wait_filled(sp, "TA", i, 1)
                    sp.dma_start(x_ln[:, :, :], x_rows(i + 1)).then_inc(sem["x_in"], 16)
                if live(i):
                    wait(sp, "x1", i - 1)
                    sp.dma_start(x_res[:, :, :], x_rows(i)).then_inc(sem["xres_in"], 16)
                    wait(sp, "q_lo", i, 3)
                    sp.wait_ge(sem["q_hi"], due("q_hi", i, 3))
                    if live(i - 1):
                        wait_filled(sp, "S", i - 1, 3)
                    for half in range(2):
                        for j in range(HC):
                            rows_j = slice(j * HD, (j + 1) * HD)
                            sp.dma_start(qx[half][rows_j, :, j, :],
                                         q_half[half][rows_j, :, :].rearrange("p c (g q) -> p (c g) q", q=N))\
                              .then_inc(sem["qx_moved"], 16)
                if live(i - 1):
                    wait(sp, "eaF", i - 2)
                    sp.dma_start(adjs["F"][:, :, :], adj_rows(i - 1)).then_inc(sem["adjF_in"], 16)
                if live(i):
                    wait(sp, "eaE", i - 1)
                    sp.dma_start(adjs["E"][:, :, :], adj_rows(i)).then_inc(sem["adjE_in"], 16)
                if live(i + 1) and live(i):
                    wait(sp, "madd", i)
                    load_adj0(i + 1)
                if live(i - 1):
                    wait(sp, "x1", i - 1)
                    wait(sp, "out_ready", i - 2)
                    if live(i - 1):
                        sp.dma_start(x1_old[:, :, :], x1_new[:, :, :]).then_inc(sem["x1_moved"], 16)
                if live(i - 2):
                    wait(sp, "out_ready", i - 2)
                    sp.dma_start(out.rearrange("b n d -> (b n) d")[bass.ds((i - 2) * UN, UN), :]
                                 .rearrange("(t p) d -> p t d", p=P), c_s["F"][:, :, :]).then_inc(sem["stored"], 16)
            iterations(sp, body)
            sp.wait_ge(sem["stored"], due("stored", U - 1))

        @block.tensor
        def _(pe):
            def transposes(i, g, stage_, src, u):
                for b, chunks in enumerate(((0, 1), (2,))):
                    wait_bank(pe, i, g, b)
                    for c in chunks:
                        for t in range(T):
                            col = (c - chunks[0]) * UN + t * P
                            last = nc.tensor.transpose(ps(g, b)[:, col:col + P], src[:, t, c * P:(c + 1) * P], ident[:, :])
                    last.then_inc(filled[g], 1)

            def project(out_ap, w, m, h_, node0, nodes, finish=None):
                n = 0
                for c in range(C):
                    for wh, hh in ((w_lo, 0), (w_hi, 1), (w_hi, 0)):
                        last = nc.tensor.matmul(out_ap, wh[:, w, c, m * P:(m + 1) * P], h_[:, c, hh, node0:node0 + nodes],
                                                start=(n == 0), stop=(n == 3 * C - 1))
                        n += 1
                return last

            def dense(out_ap, w, h_, t, bias=None):
                if bias is not None:
                    nc.tensor.matmul(out_ap, ones2[:, :], bias2[:, bias, :], start=True, stop=False)
                n = 0
                for c in range(C):
                    for hh, wh in ((1, w_hi), (0, w_lo), (0, w_hi)):
                        last = nc.tensor.matmul(out_ap, h_[:, c, hh, t * P:(t + 1) * P], wh[:, w, c, :],
                                                start=(n == 0 and bias is None), stop=(n == 3 * C - 1))
                        n += 1
                return last

            def similarity(i, g, stage_):
                wait_bank(pe, i, g, 0)
                h_ = hT[stage_]
                for t in range(T):
                    tile = slice(t * P, (t + 1) * P)
                    both = ps(g, 0)[:, t * 2 * P:(t + 1) * 2 * P]
                    cross = ps(g, 0)[:, t * 2 * P + P:(t + 1) * 2 * P]
                    for c in range(C):
                        nc.tensor.matmul(both, h_[:, c, 0, tile], h_[:, c, :, tile], start=(c == 0), stop=False)
                        last = nc.tensor.matmul(cross, h_[:, c, 1, tile], h_[:, c, 0, tile], start=False, stop=(c == C - 1))
                last.then_inc(filled[g], 1)

            def weigh(i, g, stage_, r, t):
                for which in range(3):
                    wait_bank(pe, i, g, 3 * t + which)
                    dense(ps(g, 3 * t + which)[:, 0:D], wround(r, which), hT[stage_], t, bias=3 * r + which)\
                        .then_inc(filled[g], 1)

            def flip_attention(i, g, stage_, u):
                wait_bank(pe, i, g, 0)
                wait(pe, "attn" + stage_, u)
                for t in range(T):
                    last = nc.tensor.transpose(ps(g, 0)[:, t * P:(t + 1) * P],
                                               attn[stage_][:, t, :, :].rearrange("p g j -> p (g j)"), ident[:, :])
                last.then_inc(filled[g], 1)

            def context(i, g, stage_, u):
                wait(pe, "masked" + stage_, u)
                for t in range(T):
                    wait_bank(pe, i, g, t)
                    wait(pe, "d_lo" + stage_, u, 2 * (t + 1))
                    wait(pe, "d_hi" + stage_, u, 2 * (t + 1))
                    n = 0
                    for side in range(2):
                        for ah, dh in ((1, 0), (0, 1), (0, 0)):
                            last = nc.tensor.matmul(ps(g, t)[:, 0:D], a_masked[:, side, ah, t, :], d_half[:, t, side, dh, :],
                                                    start=(n == 0), stop=(n == 5))
                            n += 1
                    last.then_inc(filled[g], 1)

            pe.wait_ge(pool_const, 4)
            pe.wait_ge(dve_const, 12)

            def body(i):
                u0, uE, uF = i, i - 1, i - 2
                if live(u0):
                    if isinstance(i, int) and i == 0:
                        pe.wait_ge(w_hi_done, 9)
                        pe.wait_ge(w_lo_done, 9)
                    wait(pe, "tA_lo", u0)
                    for b in range(3):
                        wait_bank(pe, i, "QK", b)
                        for part in range(2):
                            m = 2 * b + part
                            last = project(ps("QK", b)[:, part * UN:(part + 1) * UN], (WQ, WK)[m // C], m % C,
                                           hT["A"], 0, UN)
                        last.then_inc(filled["QK"], 1)
                if live(uF):
                    wait(pe, "zE", uF)
                    transposes(i, "TF", "F", c_s["E"], uF)
                if live(uE):
                    wait(pe, "z1", uE)
                    transposes(i, "TE", "E", z1, uE)
                if live(u0):
                    for t in range(T):
                        wait_bank(pe, i, "V", t)
                        dense(ps("V", t)[:, 0:D], WV, hT["A"], t).then_inc(filled["V"], 1)
                if live(uF):
                    wait(pe, "tF_lo", uF)
                    wait(pe, "tF_hi", uF)
                    similarity(i, "UF", "F")
                if live(uE):
                    wait(pe, "tE_lo", uE)
                    similarity(i, "UE", "E")
                if live(uF):
                    weigh(i, "DF", "F", 1, 0)
                    flip_attention(i, "AF", "F", uF)
                    weigh(i, "DF", "F", 1, 1)
                if live(u0):
                    wait(pe, "qx_moved", u0)
                    wait(pe, "q_lo", u0)
                    for t in range(T):
                        for b in range(2):
                            wait_bank(pe, i, "S", 2 * t + b)
                            for pp in range(BP):
                                pair = BP * b + pp
                                c, slot = pair // 2, 2 * (pair % 2)
                                for g in range(G):
                                    graph = G * t + g
                                    dst = ps("S", 2 * t + b)[:, (pp * G + g) * N:(pp * G + g + 1) * N]
                                    for n, (qh, kh) in enumerate(((1, 0), (0, 1), (0, 0))):
                                        last = nc.tensor.matmul(
                                            dst, qx[qh][:, c * UG + graph, slot:slot + 2, :].rearrange("p h q -> p (h q)"),
                                            k_half[kh][:, c, graph * N:(graph + 1) * N], start=(n == 0), stop=(n == 2))
                            last.then_inc(filled["S"], 1)
                if live(uF):
                    context(i, "CF", "F", uF)
                if live(uE):
                    weigh(i, "DE", "E", 0, 0)
                    flip_attention(i, "AE", "E", uE)
                    weigh(i, "DE", "E", 0, 1)
                if live(u0):
                    for t in range(T):
                        wait(pe, "exp0", u0, t + 1)
                        for b in range(2):
                            wait_bank(pe, i, "P", 2 * t + b)
                            for pp in range(BP):
                                last = nc.tensor.transpose(ps("P", 2 * t + b)[:, pp * P:(pp + 1) * P],
                                                           s[:, t, BP * b + pp, :], ident[:, :])
                            last.then_inc(filled["P"], 1)
                if live(uE):
                    context(i, "CE", "E", uE)
                if live(i + 1):
                    wait(pe, "z0", i + 1)
                    transposes(i, "TA", "A", x_ln, i + 1)
                if live(u0):
                    wait(pe, "v_lo", u0)
                    for t in range(T):
                        wait_bank(pe, i, "O", t)
                        wait(pe, "p_lo", u0, 4 * (t + 1))
                        for h in range(H):
                            for n, (ph, vh) in enumerate(((1, 0), (0, 1), (0, 0))):
                                last = nc.tensor.matmul(ps("O", t)[:, h * VC:(h + 1) * VC],
                                                        px[ph][:, t, h, :, :].rearrange("p g q -> p (g q)"),
                                                        v_half[vh][:, t, h, :], start=(n == 0), stop=(n == 2))
                        last.then_inc(filled["O"], 1)

            iterations(pe, body)

        @block.scalar
        def _(act):
            for n in range(9):
                act.wait_ge(w_in[n % 3], 16 * (n // 3 + 1))
                nc.scalar.copy(w_hi[:, n, :, :], w_stage[n % 3]).then_inc(w_hi_done, 1)
            act.wait_ge(const_in, 80)

            def relu_hi(g, stage_, u, hi_name):
                for b, chunks in enumerate(((0, 1), (2,))):
                    wait_filled(act, g, u, b)
                    nc.scalar.activation(hT[stage_][:, chunks[0]:chunks[-1] + 1, 0, :],
                                         ps(g, b)[:, 0:len(chunks) * UN].rearrange("p (c n) -> p c n", n=UN),
                                         ACT.Relu).then_inc(sem[hi_name], 1)

            def weigh_hi(g, stage_, u, t):
                for which in range(3):
                    wait_filled(act, g, u, 3 * t + which)
                    src = ps(g, 3 * t + which)[:, 0:D]
                    if which == 1:
                        if stage_ == "E":
                            wait(act, "c_readyF", u - 1, t + 1)
                        else:
                            wait(act, "c_readyE", u, t + 1)
                        nc.scalar.copy(hs[:, t, :], src).then_inc(sem["hs" + stage_], 1)
                    else:
                        nc.scalar.copy(d_half[:, t, which // 2, 0, :], src).then_inc(sem["d_hi" + stage_], 1)

            def similarity_hi(g, stage_, u):
                wait_filled(act, g, u, 0)
                v = ps(g, 0)[:, :].rearrange("p (t x j) -> p t x j", t=T, x=2)
                for gr in range(G):
                    own = slice(gr * N, (gr + 1) * N)
                    nc.scalar.copy(u_s[stage_][own, :, :], v[own, :, 0, own]).then_inc(sem["u_hh" + stage_], 1)

            def similarity_exp(stage_, u):
                wait(act, "u_sub" + stage_, u)
                nc.scalar.activation(u_s[stage_][:, :, :], u_s[stage_][:, :, :], ACT.Exp, scale=float(D) ** -0.5)\
                    .then_inc(sem["exp" + stage_], 1)

            def flip_hi(g, stage_, u):
                wait_filled(act, g, u, 0)
                nc.scalar.copy(a_half[:, 0, :, :], ps(g, 0)[:, 0:T * P].rearrange("p (t i) -> p t i", t=T))\
                    .then_inc(sem["a_hi" + stage_], 1)

            def body(i):
                u0, uE, uF = i, i - 1, i - 2
                if live(u0):
                    for m in range(2 * C):
                        if m % 2 == 0:
                            wait_filled(act, "QK", u0, m // 2)
                        dst = (q_half, k_half)[m // C][0]
                        nc.scalar.activation(dst[:, m % C, :], ps("QK", m // 2)[:, (m % 2) * UN:(m % 2 + 1) * UN],
                                             ACT.Identity, bias=param_cols[:, m // C, m % C:m % C + 1])\
                            .then_inc(sem["q_hi"], 1)
                if live(uF):
                    wait(act, "x1", u0 - 1)
                    for c in range(C):
                        if c != 1:
                            wait_filled(act, "TF", uF, c // 2)
                        src = ps("TF", c // 2)[:, (c % 2) * UN:(c % 2 + 1) * UN]
                        scale, shift = param_cols[:, 2, c:c + 1], param_cols[:, 3, c:c + 1]
                        nc.scalar.activation(hT_full[:, c, :], src, ACT.Relu, bias=shift, scale=scale)\
                            .then_inc(sem["tF_full"], 1)
                        nc.scalar.activation(hT["F"][:, c, 0, :], src, ACT.Relu, bias=shift, scale=scale)\
                            .then_inc(sem["tF_hi"], 1)
                if live(uE):
                    relu_hi("TE", "E", uE, "tE_hi")
                if live(u0):
                    for t in range(T):
                        wait_filled(act, "V", u0, t)
                        nc.scalar.copy(v_half[0][:, t, :, 0:HD], ps("V", t)[:, 0:D].rearrange("p (h d) -> p h d", h=H))\
                            .then_inc(sem["v_hi"], 1)
                if live(uF):
                    similarity_hi("UF", "F", uF)
                if live(uE):
                    similarity_hi("UE", "E", uE)
                if live(uF):
                    similarity_exp("F", uF)
                    weigh_hi("DF", "F", uF, 0)
                if live(uE):
                    similarity_exp("E", uE)
                if live(uF):
                    flip_hi("AF", "F", uF)
                    weigh_hi("DF", "F", uF, 1)
                if live(uE):
                    weigh_hi("DE", "E", uE, 0)
                if live(u0):
                    exp_scores(u0, 0)
                if live(uE):
                    flip_hi("AE", "E", uE)
                if live(u0):
                    exp_scores(u0, 1)
                if live(uE):
                    weigh_hi("DE", "E", uE, 1)
                if live(u0):
                    for n in range(2 * T):
                        wait_filled(act, "P", u0, n)
                        t, b = n // 2, n % 2
                        for g in range(G):
                            own = slice(g * N, (g + 1) * N)
                            nc.scalar.copy(px[0][own, t, 2 * BP * b:2 * BP * (b + 1), g, :],
                                           ps("P", n)[own, 0:BP * P].rearrange("p (h q) -> p h q", q=N))\
                                .then_inc(sem["p_hi"], 1)
                if live(i + 1):
                    relu_hi("TA", "A", i + 1, "tA_hi")

            def exp_scores(u, t):
                wait(act, "s_sub", u, t + 1)
                nc.scalar.activation(s[:, t, :, :], s[:, t, :, :], ACT.Exp).then_inc(sem["exp0"], 1)

            iterations(act, body)

        @block.gpsimd
        def _(pool):
            nc.gpsimd.memset(ident[:, :], 0.0)
            nc.gpsimd.memset(later[:, :], 0.0)
            nc.gpsimd.memset(half_power[:, :], -0.5)
            nc.gpsimd.memset(earlier[:, :], 0.0).then_inc(pool_const, 1)
            pool.wait_ge(pool_const, 1)
            for g in range(G):
                own = slice(g * N, (g + 1) * N)
                nc.gpsimd.memset(later[own, own], 1.0)
                last = nc.gpsimd.memset(earlier[own, own], 1.0)
            last.then_inc(pool_const, 1)
            pool.wait_ge(pool_const, 2)
            nc.gpsimd.affine_select(out=ident[:, :], in_=ident[:, :], compare_op=ALU.not_equal, fill=1.0,
                                    base=0, pattern=[[-1, P]], channel_multiplier=1)
            nc.gpsimd.affine_select(out=later[:, :], in_=later[:, :], compare_op=ALU.is_gt, fill=0.0,
                                    base=0, pattern=[[-1, P]], channel_multiplier=1)
            nc.gpsimd.affine_select(out=earlier[:, :], in_=earlier[:, :], compare_op=ALU.is_gt, fill=0.0,
                                    base=0, pattern=[[1, P]], channel_multiplier=-1).then_inc(pool_const, 2)
            pool.wait_ge(const_in, 80)

            def inverse_root(which, u):
                wait(pool, "ve" + which, u)
                nc.gpsimd.tensor_tensor(rstd[which][:, :], ve[which][:, :], half_power[:, :], ALU.pow)\
                    .then_inc(sem["rstd" + which], 1)

            def weigh_adjacency(stage_, u):
                wait(pool, "adj" + stage_ + "_in", u)
                wait(pool, "exp" + stage_, u)
                nc.gpsimd.tensor_tensor(ea[stage_][:, :, :], u_s[stage_][:, :, :], adjs[stage_][:, :, :], ALU.mult)\
                    .then_inc(sem["ea" + stage_], 1)

            def diagonal(stage_, u):
                wait(pool, "attn" + stage_, u)
                nc.gpsimd.tensor_tensor(u_s[stage_][:, :, :], attn[stage_][:, :, 0, :],
                                        eye[:, :].unsqueeze(1).to_broadcast([P, T, N]), ALU.mult)\
                    .then_inc(sem["de" + stage_], 1)

            def mask(stage_, u):
                wait(pool, "a_lo" + stage_, u)
                wait(pool, "a_hi" + stage_, u)
                src = a_half[:, :, :, :].rearrange("p x t i -> p (x t) i").bitcast(F32)
                for side, m in enumerate((later, earlier)):
                    nc.gpsimd.tensor_tensor(a_masked[:, side, :, :, :].rearrange("p x t i -> p (x t) i"), src,
                                            m[:, :].unsqueeze(1).to_broadcast([P, 2 * T, P]), ALU.mult)\
                        .then_inc(sem["masked" + stage_], 1)

            def body(i):
                u0, uE, uF = i, i - 1, i - 2
                if live(u0):
                    wait(pool, "xres_in", u0)
                    nc.gpsimd.tensor_tensor(x_res[:, :, :], x_res[:, :, :],
                                            param_rows[:, 0:1, :].to_broadcast([P, T, D]), ALU.add)\
                        .then_inc(sem["xb"], 1)
                if live(uF):
                    wait(pool, "tF_full", uF)
                    wait(pool, "tF_hi", uF)
                    nc.gpsimd.tensor_tensor(hT["F"][:, :, 1, :], hT_full[:, :, :],
                                            hT["F"][:, :, 0, :].bitcast(F32), ALU.subtract).then_inc(sem["tF_lo"], 1)
                    weigh_adjacency("F", uF)
                if live(uE):
                    weigh_adjacency("E", uE)
                if live(uF):
                    diagonal("F", uF)
                    mask("F", uF)
                if live(uE):
                    diagonal("E", uE)
                if live(i + 1):
                    inverse_root("0", i + 1)
                if live(u0):
                    for t in range(T):
                        wait(pool, "s_max", u0, t + 1)
                        nc.gpsimd.tensor_tensor(
                            s[:, t, :, :].rearrange("p a (g k) -> p (a g) k", k=N),
                            s[:, t, :, :].rearrange("p a (g k) -> p (a g) k", k=N),
                            s_max[:, t, :].unsqueeze(2).to_broadcast([P, PAIRS * G, N]), ALU.subtract)\
                            .then_inc(sem["s_sub"], 1)
                if live(uF):
                    inverse_root("F", uF)
                if live(uE):
                    mask("E", uE)
                if live(uF):
                    for t in range(T):
                        wait(pool, "zF", uF, t + 1)
                        nc.gpsimd.tensor_tensor(c_s["F"][:, t, :], c_s["F"][:, t, :], param_rows[:, 1, :], ALU.mult)\
                            .then_inc(sem["yg"], 1)
                        wait(pool, "yg", uF, t + 1)
                        nc.gpsimd.tensor_tensor(c_s["F"][:, t, :], c_s["F"][:, t, :], param_rows[:, 2, :], ALU.add)\
                            .then_inc(sem["yb"], 1)
                if live(uE):
                    inverse_root("E", uE)
                if live(u0):
                    wait(pool, "x1_moved", u0 - 1)
                    wait(pool, "xb", u0)
                    for t in range(T):
                        wait(pool, "o_ready", u0, t + 1)
                        nc.gpsimd.tensor_tensor(x1_new[:, t, :], o[:, t, :], x_res[:, t, :], ALU.add)\
                            .then_inc(sem["x1"], 1)
                    inverse_root("1", u0)

            iterations(pool, body)

        @block.vector
        def _(dve):
            for n in range(9):
                dve.wait_ge(w_hi_done, n + 1)
                nc.vector.tensor_tensor(w_lo[:, n, :, :], w_stage[n % 3], w_hi[:, n, :, :].bitcast(F32), ALU.subtract)\
                    .then_inc(w_lo_done, 1)
            dve.wait_ge(w_lo_done, 9)
            dve.wait_ge(const_in, 80)
            dve.wait_ge(pool_const, 4)
            n = 0
            for r in range(2):
                both = bias2[:, 3 * r:3 * r + 3, :]
                steps = (
                    lambda: nc.vector.tensor_copy(both, bias_raw[r]),
                    lambda: nc.vector.tensor_tensor(bias_raw[r], bias_raw[r], both.bitcast(F32), ALU.subtract),
                    lambda: nc.vector.tensor_scalar(bias_raw[r], bias_raw[r], ident[0:2, 1:2], None, ALU.mult),
                    lambda: nc.vector.scalar_tensor_tensor(both, both.bitcast(F32), ident[0:2, 0:1], bias_raw[r],
                                                           ALU.mult, ALU.add),
                )
                for step in steps:
                    step().then_inc(dve_const, 1)
                    n += 1
                    dve.wait_ge(dve_const, n)
            nc.vector.memset(ones2[:, :].bitcast(F32), 1.0).then_inc(dve_const, 1)
            nc.vector.tensor_tensor(eye[:, :], ident[:, 0:N], ident[:, N:P], ALU.add).then_inc(dve_const, 1)
            for half in range(2):
                nc.vector.memset(qx[half][:, :, :, :], 0.0)
                nc.vector.memset(v_half[half][:, :, :, HD:VC], 1.0 - half)
                last = nc.vector.memset(px[half][:, :, :, :, :], 0.0)
                last.then_inc(dve_const, 1)

            def norm_stats(which, u, srcs, names):
                eps = LN_EPS["01EF".index(which)]
                for t in range(T):
                    if names:
                        wait(dve, names, u, None if COUNTS[names] != T else t + 1)
                    nc.vector.bn_stats(stats[which][:, t, :], srcs[:, t, :]).then_inc(sem["stats" + which], 1)
                wait(dve, "stats" + which, u)
                nc.vector.memset(ve[which][:, :], eps)
                for t in range(T):
                    nc.vector.bn_aggr(mv[which][:, t, :], stats[which][:, t, :]).then_inc(sem["mv" + which], 1)
                wait(dve, "mv" + which, u)
                nc.vector.tensor_tensor(ve[which][:, :], ve[which][:, :], mv[which][:, :, 1], ALU.add)\
                    .then_inc(sem["ve" + which], 1)

            def norm_apply(which, u, dst, srcs, name):
                wait(dve, "rstd" + which, u)
                for t in range(T):
                    nc.vector.tensor_scalar(dst[:, t, :], srcs[:, t, :], mv[which][:, t, 0:1], rstd[which][:, t:t + 1],
                                            ALU.subtract, ALU.mult).then_inc(sem[name], 1)

            def relu_lo(g, stage_, u, hi_name, lo_name):
                for b, chunks in enumerate(((0, 1), (2,))):
                    wait(dve, hi_name, u, b + 1)
                    span = slice(chunks[0], chunks[-1] + 1)
                    nc.vector.scalar_tensor_tensor(hT[stage_][:, span, 1, :],
                                                   ps(g, b)[:, 0:len(chunks) * UN].rearrange("p (c n) -> p c n", n=UN), 0.0,
                                                   hT[stage_][:, span, 0, :].bitcast(F32), ALU.max, ALU.subtract)\
                        .then_inc(sem[lo_name], 1)

            def similarity_softmax_1(g, stage_, u):
                wait(dve, "u_hh" + stage_, u)
                v = ps(g, 0)[:, :].rearrange("p (t x j) -> p t x j", t=T, x=2)
                for gr in range(G):
                    own = slice(gr * N, (gr + 1) * N)
                    nc.vector.tensor_tensor(u_s[stage_][own, :, :], v[own, :, 1, own], u_s[stage_][own, :, :], ALU.add)\
                        .then_inc(sem["u_sum" + stage_], 1)
                wait(dve, "u_sum" + stage_, u)
                nc.vector.tensor_reduce(u_max[stage_][:, :], u_s[stage_][:, :, :], AX_X, ALU.max)\
                    .then_inc(sem["u_max" + stage_], 1)
                wait(dve, "u_max" + stage_, u)
                nc.vector.tensor_tensor(u_s[stage_][:, :, :], u_s[stage_][:, :, :],
                                        u_max[stage_][:, :].unsqueeze(2).to_broadcast([P, T, N]), ALU.subtract)\
                    .then_inc(sem["u_sub" + stage_], 1)

            def similarity_softmax_2(stage_, u):
                wait(dve, "exp" + stage_, u)
                nc.vector.tensor_reduce(esum[stage_][:, :], u_s[stage_][:, :, :], AX_X, ALU.add)\
                    .then_inc(sem["esum" + stage_], 1)
                wait(dve, "ea" + stage_, u)
                nc.vector.tensor_reduce(easum[stage_][:, :], ea[stage_][:, :, :], AX_X, ALU.add)\
                    .then_inc(sem["easum" + stage_], 1)
                wait(dve, "esum" + stage_, u)
                wait(dve, "easum" + stage_, u)
                nc.vector.scalar_tensor_tensor(den[stage_][:, :], esum[stage_][:, :], 1e-10, easum[stage_][:, :],
                                               ALU.mult, ALU.add).then_inc(sem["den" + stage_], 1)
                wait(dve, "den" + stage_, u)
                nc.vector.reciprocal(rden[stage_][:, :], den[stage_][:, :]).then_inc(sem["rden" + stage_], 1)
                wait(dve, "rden" + stage_, u)
                nc.vector.tensor_tensor(attn[stage_][:, :, :, :],
                                        ea[stage_][:, :, :].unsqueeze(2).to_broadcast([P, T, G, N]),
                                        rden[stage_][:, :].unsqueeze(2).unsqueeze(3).to_broadcast([P, T, G, N]), ALU.mult)\
                    .then_inc(sem["attn" + stage_], 1)

            def diagonal_sum(stage_, u):
                wait(dve, "de" + stage_, u)
                nc.vector.tensor_reduce(diag[stage_][:, :], u_s[stage_][:, :, :], AX_X, ALU.add)\
                    .then_inc(sem["diag" + stage_], 1)

            def weigh_lo(g, stage_, u, t):
                for side in range(2):
                    wait(dve, "d_hi" + stage_, u, 2 * t + side + 1)
                    nc.vector.tensor_tensor(d_half[:, t, side, 1, :], ps(g, 3 * t + 2 * side)[:, 0:D],
                                            d_half[:, t, side, 0, :].bitcast(F32), ALU.subtract)\
                        .then_inc(sem["d_lo" + stage_], 1)

            def flip_lo(g, stage_, u):
                wait(dve, "a_hi" + stage_, u)
                nc.vector.tensor_tensor(a_half[:, 1, :, :], ps(g, 0)[:, 0:T * P].rearrange("p (t i) -> p t i", t=T),
                                        a_half[:, 0, :, :].bitcast(F32), ALU.subtract).then_inc(sem["a_lo" + stage_], 1)

            def add_same(g, stage_, u):
                wait(dve, "diag" + stage_, u)
                wait(dve, "hs" + stage_, u)
                if stage_ == "F":
                    wait(dve, "stored", u - 1)
                for t in range(T):
                    wait_filled(dve, g, u, t)
                    nc.vector.scalar_tensor_tensor(c_s[stage_][:, t, :], hs[:, t, :], diag[stage_][:, t:t + 1],
                                                   ps(g, t)[:, 0:D], ALU.mult, ALU.add)\
                        .then_inc(sem["c_ready" + stage_], 1)

            def body(i):
                u0, uE, uF = i, i - 1, i - 2
                if live(u0):
                    for m in range(2 * C):
                        wait(dve, "q_hi", u0, 2 * (m // 2) + 2)
                        half = (q_half, k_half)[m // C]
                        nc.vector.scalar_tensor_tensor(half[1][:, m % C, :],
                                                       ps("QK", m // 2)[:, (m % 2) * UN:(m % 2 + 1) * UN],
                                                       param_cols[:, m // C, m % C:m % C + 1], half[0][:, m % C, :],
                                                       ALU.add, ALU.subtract).then_inc(sem["q_lo"], 1)
                if live(uE):
                    relu_lo("TE", "E", uE, "tE_hi", "tE_lo")
                if live(u0):
                    for t in range(T):
                        wait(dve, "v_hi", u0, t + 1)
                        nc.vector.tensor_tensor(v_half[1][:, t, :, 0:HD], ps("V", t)[:, 0:D].rearrange("p (h d) -> p h d", h=H),
                                                v_half[0][:, t, :, 0:HD], ALU.subtract).then_inc(sem["v_lo"], 1)
                if live(uF):
                    similarity_softmax_1("UF", "F", uF)
                if live(uE):
                    similarity_softmax_1("UE", "E", uE)
                if live(uF):
                    similarity_softmax_2("F", uF)
                    weigh_lo("DF", "F", uF, 0)
                if live(uE):
                    similarity_softmax_2("E", uE)
                if live(uF):
                    diagonal_sum("F", uF)
                    flip_lo("AF", "F", uF)
                    weigh_lo("DF", "F", uF, 1)
                if live(uE):
                    diagonal_sum("E", uE)
                if live(i + 1):
                    norm_stats("0", i + 1, x_ln, "x_in")
                if live(u0):
                    wait(dve, "adj0_in", u0)
                    nc.vector.tensor_scalar(madd[:, :, :], adj0[:, :, :], 0.0, MASKED, ALU.is_le, ALU.mult)\
                        .then_inc(sem["s_t"], 1)
                    wait(dve, "s_t", u0)
                    nc.vector.scalar_tensor_tensor(madd[:, :, :], adj0[:, :, :], beta_col[:, 0:1], madd[:, :, :],
                                                   ALU.mult, ALU.add).then_inc(sem["madd"], 1)
                    wait(dve, "madd", u0)
                    for t in range(T):
                        for b in range(2):
                            wait_filled(dve, "S", u0, 2 * t + b)
                            nc.vector.scalar_tensor_tensor(
                                s[:, t, BP * b:BP * (b + 1), :],
                                ps("S", 2 * t + b)[:, 0:BP * P].rearrange("p (a k) -> p a k", a=BP), float(HD) ** -0.5,
                                madd[:, G * t:G * (t + 1), :].rearrange("p g k -> p (g k)").unsqueeze(1)
                                .to_broadcast([P, BP, P]), ALU.mult, ALU.add).then_inc(sem["s_sum"], 1)
                        wait(dve, "s_sum", u0, 2 * (t + 1))
                        nc.vector.tensor_reduce(s_max[:, t, :], s[:, t, :, :].rearrange("p a (g k) -> p (a g) k", k=N),
                                                AX_X, ALU.max).then_inc(sem["s_max"], 1)
                if live(i + 1):
                    norm_apply("0", i + 1, x_ln, x_ln, "z0")
                if live(uF):
                    add_same("CF", "F", uF)
                    norm_stats("F", uF, c_s["F"], "c_readyF")
                if live(uE):
                    weigh_lo("DE", "E", uE, 0)
                if live(uF):
                    norm_apply("F", uF, c_s["F"], c_s["F"], "zF")
                if live(uE):
                    flip_lo("AE", "E", uE)
                    weigh_lo("DE", "E", uE, 1)
                if live(u0):
                    for n in range(2 * T):
                        t, b = n // 2, n % 2
                        wait(dve, "p_hi", u0, 2 * n + 2)
                        for g in range(G):
                            own = slice(g * N, (g + 1) * N)
                            at = (own, t, slice(2 * BP * b, 2 * BP * (b + 1)), g)
                            nc.vector.tensor_tensor(px[1][at], ps("P", n)[own, 0:BP * P].rearrange("p (h q) -> p h q", q=N),
                                                    px[0][at], ALU.subtract).then_inc(sem["p_lo"], 1)
                if live(uF):
                    wait(dve, "x1_moved", uF)
                    for t in range(T):
                        wait(dve, "yb", uF, t + 1)
                        nc.vector.scalar_tensor_tensor(c_s["F"][:, t, :], c_s["F"][:, t, :], 0.0, x1_old[:, t, :],
                                                       ALU.max, ALU.add).then_inc(sem["out_ready"], 1)
                if live(uE):
                    add_same("CE", "E", uE)
                    norm_stats("E", uE, c_s["E"], "c_readyE")
                if live(i + 1):
                    relu_lo("TA", "A", i + 1, "tA_hi", "tA_lo")
                if live(uE):
                    norm_apply("E", uE, c_s["E"], c_s["E"], "zE")
                if live(u0):
                    wait(dve, "tF_lo", uF)
                    for t in range(T):
                        wait_filled(dve, "O", u0, t)
                        v = ps("O", t)[:, 0:H * VC].rearrange("p (h c) -> p h c", c=VC)
                        nc.vector.reciprocal(o_rsum[:, t, :], v[:, :, HD]).then_inc(sem["osum"], 1)
                        wait(dve, "osum", u0, t + 1)
                        nc.vector.tensor_tensor(o[:, t, :].rearrange("p (h d) -> p h d", h=H), v[:, :, 0:HD],
                                                o_rsum[:, t, :].unsqueeze(2).to_broadcast([P, H, HD]), ALU.mult)\
                            .then_inc(sem["o_ready"], 1)
                    norm_stats("1", u0, x1_new, "x1")
                    norm_apply("1", u0, z1, x1_new, "z1")

            iterations(dve, body)


def kernel(x, adj, L0_gnn_Wq, L0_gnn_bq, L0_gnn_Wk, L0_gnn_bk, L0_gnn_Wv, L0_gnn_bv, L0_gnn_beta, L1_gnn_Wl, L1_gnn_bl,
           L1_gnn_Ws, L1_gnn_bs, L1_gnn_Wr, L1_gnn_br, L1_gnn_ln_w, L1_gnn_ln_b):
    import numpy as np
    import concourse.bacc as bacc
    from concourse.bass_utils import run_bass_kernel_spmd

    rounds = [np.asarray(w)[r].T for r in range(2) for w in (L1_gnn_Wl, L1_gnn_Ws, L1_gnn_Wr)]
    by_feature = [L0_gnn_bq, L0_gnn_bk, L1_gnn_ln_w[0], L1_gnn_ln_b[0]]
    arrays = {
        "x": np.asarray(x), "adj": np.asarray(adj),
        "weights": np.stack([np.asarray(w) for w in (L0_gnn_Wq, L0_gnn_Wk, L0_gnn_Wv)] + rounds),
        "cols": np.stack([np.asarray(b) for b in by_feature]).reshape(4, C, P).transpose(2, 0, 1),
        "rows": np.concatenate([np.asarray(b) for b in (L0_gnn_bv, L1_gnn_ln_w[1], L1_gnn_ln_b[1])]),
        "biases": np.concatenate([np.asarray(b)[r] for r in range(2) for b in (L1_gnn_bl, L1_gnn_bs, L1_gnn_br)])
                    .reshape(2, 3, D),
        "beta": np.asarray(L0_gnn_beta).reshape(1),
    }
    arrays = {n: np.ascontiguousarray(a) for n, a in arrays.items()}
    nc = bacc.Bacc("TRN2", target_bir_lowering=False, num_devices=1)
    args = [nc.dram_tensor(n, a.shape, mybir.dt.from_np(a.dtype), kind="ExternalInput").ap() for n, a in arrays.items()]
    out = nc.dram_tensor("out", arrays["x"].shape, F32, kind="ExternalOutput").ap()
    build(nc, *args, out)
    return run_bass_kernel_spmd(nc, [arrays], core_ids=[0]).results[0]["out"]
```

```python
from contextlib import ExitStack

import concourse.bass as bass
from concourse import mybir

ALU = mybir.AluOpType
ACT = mybir.ActivationFunctionType
F32 = mybir.dt.float32
F32R = mybir.dt.float32r
F16 = mybir.dt.float16
AX_X = mybir.AxisListType.X

P = 128
N = 64
G = P // N
T = 2
UN = T * P
UG = T * G
D = 384
C = D // P
H = 12
HD = D // H
HC = H // C
PAIRS = H // 2
BP = PAIRS // 2
VC = HD + 1
BANK = 512

LN_EPS = (1e-5, 1e-5, 1e-12, 1e-12)
MASKED = -9000000000000000.0

WQ, WK, WV = 0, 1, 2


def wround(r, which):
    return 3 + 3 * r + which


FILLS = (
    [("QK", k) for k in range(3)] + [("TE", 0), ("TE", 1)]
    + [("TF", 0), ("TF", 1), ("V", 0), ("V", 1), ("UE", 0), ("UF", 0)] + [("S", k) for k in range(4)]
    + [("DF", k) for k in range(3)] + [("AF", 0)] + [("DF", k) for k in range(3, 6)]
    + [("P", k) for k in range(4)] + [("TA", 0), ("TA", 1)]
    + [("DE", k) for k in range(3)] + [("CF", 0), ("CF", 1), ("AE", 0)] + [("DE", k) for k in range(3, 6)]
    + [("O", 0), ("O", 1), ("CE", 0), ("CE", 1)]
)
PER = {}
for _g, _k in FILLS:
    PER[_g] = PER.get(_g, 0) + 1
LAG = {"QK": 0, "V": 0, "S": 0, "P": 0, "O": 0, "TA": -1,
       "TE": 1, "UE": 1, "DE": 1, "AE": 1, "CE": 1,
       "TF": 2, "UF": 2, "DF": 2, "AF": 2, "CF": 2}


def banks():
    out, n = {}, 0
    for fill in FILLS:
        if fill[0] == "AF":
            out[fill] = (n + 4) % 8
        else:
            out[fill] = n % 8
            n += 1
    return out


BANK_OF = banks()

COUNTS = {
    "x_in": 16, "xres_in": 16, "adj0_in": 32, "adjE_in": 16, "adjF_in": 16,
    "qx_moved": 16 * HC, "x1_aged": 16, "x1_moved": 16, "stored": 16,
    "z0": 2, "z1": 2, "zE": 2, "q_hi": 6, "tA_hi": 2, "tA_full": 2, "tE_hi": 2, "tF_hi": 3, "tF_full": 3, "v_hi": 2,
    "u_hhE": 2, "u_hhF": 2, "expE": 1, "expF": 1, "d_hiE": 4, "d_hiF": 4,
    "a_hiE": 1, "a_hiF": 1, "exp0": 2, "p_hi": 8,
    "q_lo": 6, "tE_lo": 2, "v_lo": 2, "a_loE": 1, "a_loF": 1, "d_fullE": 4, "d_fullF": 4, "hsE": 2, "hsF": 2,
    "u_sumE": 2, "u_sumF": 2, "u_maxE": 1, "u_maxF": 1, "u_subE": 1, "u_subF": 1,
    "esumE": 1, "esumF": 1, "easumE": 1, "easumF": 1, "denE": 1, "denF": 1, "rdenE": 1, "rdenF": 1,
    "attnE": 1, "attnF": 1, "deE": 1, "deF": 1, "diagE": 1, "diagF": 1,
    "s_t": 1, "madd": 1, "s_sum": 4, "s_max": 2, "p_lo": 8, "osum": 2, "o_ready": 2,
    "c_readyE": 2, "c_readyF": 2, "yg": 2, "yb": 2, "out_ready": 2,
    "stats0": 2, "stats1": 2, "statsE": 2, "statsF": 2,
    "neg_mean0": 1, "neg_mean1": 1, "neg_meanE": 1, "mv0": 2, "mv1": 2, "mvE": 2, "mvF": 2,
    "ve0": 1, "ve1": 1, "veE": 1, "veF": 1,
    "d_loE": 4, "d_loF": 4, "tF_lo": 3, "tA_lo": 2, "eaE": 1, "eaF": 1, "maskedE": 2, "maskedF": 2,
    "shift0": 1, "shift1": 1, "shiftE": 1, "rstd0": 1, "rstd1": 1, "rstdE": 1, "rstdF": 1,
    "xb": 1, "s_sub": 2, "x1": 2,
}


def build(nc, x, adj, weights, cols, rows, biases, beta, out):
    U = x.shape[0] // UG
    ctx = ExitStack()
    with ctx:
        def sb(name, shape, dt=F32):
            return ctx.enter_context(nc.sbuf_tensor(name, shape, dt))

        w_hi = sb("w_hi", [P, 9, C, D], F32R)
        w_lo = sb("w_lo", [P, 9, C, D], F32R)
        param_cols = sb("param_cols", [P, 4, C])
        param_rows = sb("param_rows", [P, 3, D])
        beta_col = sb("beta_col", [P, 1])
        bias_rows = sb("bias_rows", [P, 6, D])
        ident = sb("ident", [P, P])
        eye = sb("eye", [P, N])
        later = sb("later", [P, P])
        earlier = sb("earlier", [P, P])
        half_power = sb("half_power", [P, T])
        x_ln = sb("x_ln", [P, T, D])
        x_res = sb("x_res", [P, T, D])
        adj0 = sb("adj0", [P, UG, N])
        madd = sb("madd", [P, UG, N])
        hT = {s: sb(f"hT_{s}", [P, C, 2, UN], F32R) for s in "AEF"}
        hT_full = sb("hT_full", [P, C, UN])
        q_both = sb("q_both", [P, 2, C, UN], F16)
        q_half = [q_both[:, half, :, :] for half in range(2)]
        k_half = [sb(f"k_{n}", [P, C, UN], F16) for n in ("hi", "lo")]
        qx_both = sb("qx_both", [P, 2 * C * UG, HC, N], F16)
        qx = [qx_both[:, half * C * UG:(half + 1) * C * UG, :, :] for half in range(2)]
        v_half = [sb(f"v_{n}", [P, T, H, VC], F16) for n in ("hi", "lo")]
        s = sb("s", [P, T, PAIRS, P])
        s_max = sb("s_max", [P, T, PAIRS * G])
        px = [sb(f"px_{n}", [P, T, H, G, N], F16) for n in ("hi", "lo")]
        o_rsum = sb("o_rsum", [P, T, H])
        o = hT_full[:, :, :].rearrange("p c n -> p (c n)").rearrange("p (t d) -> p t d", t=T)
        x1_mid = sb("x1_mid", [P, T, D])
        x1_old = sb("x1_old", [P, T, D])
        z1 = sb("z1", [P, T, D])
        adjs = {s_: sb(f"adj_{s_}", [P, T, N]) for s_ in "EF"}
        u_s = {s_: sb(f"u_{s_}", [P, T, N]) for s_ in "EF"}
        u_max = {s_: sb(f"u_max_{s_}", [P, T]) for s_ in "EF"}
        ea = {s_: sb(f"ea_{s_}", [P, T, N]) for s_ in "EF"}
        esum = {s_: sb(f"esum_{s_}", [P, T]) for s_ in "EF"}
        easum = {s_: sb(f"easum_{s_}", [P, T]) for s_ in "EF"}
        den = {s_: sb(f"den_{s_}", [P, T]) for s_ in "EF"}
        rden = {s_: sb(f"rden_{s_}", [P, T]) for s_ in "EF"}
        diag = {s_: sb(f"diag_{s_}", [P, T]) for s_ in "EF"}
        attn = {s_: sb(f"attn_{s_}", [P, T, G, N]) for s_ in "EF"}
        a_half = sb("a_half", [P, 2, T, P], F32R)
        a_masked = sb("a_masked", [P, 2, 2, T, P], F32R)
        d_half = sb("d_half", [P, T, 2, 2, D], F32R)
        d_full = sb("d_full", [P, 2, D])
        c_s = {s_: sb(f"c_{s_}", [P, T, D]) for s_ in "EF"}
        stats = {s_: sb(f"stats_{s_}", [P, T, 6]) for s_ in "01EF"}
        mv = {s_: sb(f"mv_{s_}", [P, T, 2]) for s_ in "01EF"}
        ve = {s_: sb(f"ve_{s_}", [P, T]) for s_ in "01EF"}
        rstd = {s_: sb(f"rstd_{s_}", [P, T]) for s_ in "01EF"}
        neg_mean = {s_: sb(f"neg_mean_{s_}", [P, T]) for s_ in "01E"}
        shift = {s_: sb(f"shift_{s_}", [P, T]) for s_ in "01E"}

        def chunks_of(*bufs):
            return [b[:, k * D:(k + 1) * D] for b in bufs for k in range(b.shape[1] // D)]
        early = chunks_of(px[0][:, :, :, :, :].rearrange("p t h g q -> p (t h g q)").bitcast(F32)[:, 0:C * D],
                          px[1][:, :, :, :, :].rearrange("p t h g q -> p (t h g q)").bitcast(F32)[:, 0:C * D],
                          qx[0].rearrange("p a b c -> p (a b c)").bitcast(F32)[:, 0:C * D])
        late = chunks_of(*(b[:, :, :].rearrange("p t d -> p (t d)") for b in (c_s["E"], c_s["F"], x1_old, x1_mid, z1)))
        w_landing = [early[n * C:(n + 1) * C] for n in range(3)] + 2 * [late[n * C:(n + 1) * C] for n in range(3)]

        bank = [ctx.enter_context(nc.psum_tensor(f"bank{b}", [P, BANK], F32)) for b in range(8)]

        sem = {n: ctx.enter_context(nc.semaphore(n)) for n in COUNTS}
        filled = {g: ctx.enter_context(nc.semaphore(f"filled_{g}")) for g in PER}
        const_in = ctx.enter_context(nc.semaphore("const_in"))
        w_in = [ctx.enter_context(nc.semaphore(f"w_in{n}")) for n in range(9)]
        bias_in = ctx.enter_context(nc.semaphore("bias_in"))
        w_hi_done = ctx.enter_context(nc.semaphore("w_hi_done"))
        w_lo_done = ctx.enter_context(nc.semaphore("w_lo_done"))
        pool_const = ctx.enter_context(nc.semaphore("pool_const"))
        zeroed = ctx.enter_context(nc.semaphore("zeroed"))
        dve_const = ctx.enter_context(nc.semaphore("dve_const"))

        def live(u):
            return not isinstance(u, int) or 0 <= u < U

        def is_first(u):
            return isinstance(u, int) and u == 0

        def due(name, u, k=None):
            return u * COUNTS[name] + (COUNTS[name] if k is None else k)

        def nth(g, u, k):
            return u * PER[g] + k + 1

        def ps(g, k):
            return bank[BANK_OF[g, k]]

        def wait_bank(pe, i, g, k):
            at = FILLS.index((g, k))
            mine = BANK_OF[g, k]
            earlier_fills = [(f, 0) for f in reversed(FILLS[:at])]
            for back in (1, 2, 3):
                earlier_fills += [(f, back) for f in reversed(FILLS)]
            for (pg, pk), back in earlier_fills:
                u = i - back - LAG[pg]
                if BANK_OF[pg, pk] == mine and live(u):
                    name, k_read = last_read(pg, pk)
                    pe.wait_ge(sem[name], due(name, u, k_read))
                    return

        def last_read(g, k):
            return {
                "QK": ("q_lo", 2 * k + 2), "V": ("v_lo", k + 1), "S": ("s_sum", k + 1),
                "P": ("p_lo", 2 * k + 2), "O": ("o_ready", k + 1), "TF": ("tF_hi", 2 + k),
                "TE": ("tE_lo", k + 1), "TA": ("tA_hi", k + 1),
                "U" + g[1:]: ("u_sum" + g[1:], 2), "A" + g[1:]: ("a_lo" + g[1:], 1),
                "D" + g[1:]: (("hs" + g[1:], k // 3 + 1) if k % 3 == 1
                              else ("d_full" + g[1:], 2 * (k // 3) + (k % 3) // 2 + 1)),
                "C" + g[1:]: ("c_ready" + g[1:], k + 1),
            }[g]

        block = ctx.enter_context(nc.Block())

        SPECIAL_FIRST = range(-1, 3)
        LOOP = (3, U - 2)
        SPECIAL_LAST = range(U - 2, U + 3)

        def iterations(eng, body):
            for i in SPECIAL_FIRST:
                body(i)
            with eng.Fori(*LOOP) as i:
                body(i)
            for i in SPECIAL_LAST:
                body(i)

        @block.sync
        def _(sp):
            def x_rows(u):
                return x.rearrange("b n d -> (b n) d")[bass.ds(u * UN, UN), :].rearrange("(t p) d -> p t d", p=P)

            def adj_rows(u):
                return adj.rearrange("b i j -> (b i) j")[bass.ds(u * UN, UN), :].rearrange("(t p) j -> p t j", p=P)

            def load_adj0(u):
                src = adj[bass.ds(u * UG, UG), :, :].rearrange("g q k -> q g k")
                for h in range(2):
                    sp.dma_start(adj0[h * N:(h + 1) * N, :, :], src).then_inc(sem["adj0_in"], 16)

            def load_weight(n):
                for c in range(C):
                    sp.dma_start(w_landing[n][c], weights[n, c * P:(c + 1) * P, :]).then_inc(w_in[n], 16)

            sp.dma_start(x_ln[:, :, :], x_rows(0)).then_inc(sem["x_in"], 16)
            for n in range(6):
                load_weight(n)
                if n == 1:
                    sp.dma_start(param_cols[:, :, :], cols).then_inc(const_in, 16)
                    sp.dma_start(param_rows[:, :, :].rearrange("p a d -> p (a d)"),
                                 rows.partition_broadcast(P)).then_inc(const_in, 16)
                    sp.dma_start(beta_col[:, :], beta.partition_broadcast(P)).then_inc(const_in, 16)
                if n == 2:
                    sp.dma_start(x_res[:, :, :], x_rows(0)).then_inc(sem["xres_in"], 16)
                    load_adj0(0)
            sp.dma_start(bias_rows[:, :, :].rearrange("p n d -> p (n d)"), biases.rearrange("n d -> (n d)")
                         .partition_broadcast(P)).then_inc(bias_in, 16)

            def body(i):
                if live(i):
                    sp.wait_ge(sem["q_lo"], due("q_lo", i, 3))
                    sp.wait_ge(sem["q_hi"], due("q_hi", i, 3))
                    if is_first(i):
                        sp.wait_ge(zeroed, 1)
                    if live(i - 1):
                        sp.wait_ge(filled["S"], nth("S", i - 1, 3))
                    for j in range(HC):
                        rows_j = slice(j * HD, (j + 1) * HD)
                        sp.dma_start(qx_both[rows_j, :, j, :],
                                     q_both[rows_j, :, :, :].rearrange("p x c (g q) -> p (x c g) q", q=N))\
                          .then_inc(sem["qx_moved"], 16)
                if is_first(i):
                    for n in range(6, 9):
                        sp.wait_ge(w_lo_done, C * (n - 2))
                        load_weight(n)
                u = i - 1
                if live(u - 2):
                    sp.wait_ge(sem["out_ready"], due("out_ready", u - 2))
                    sp.dma_start(out.rearrange("b n d -> (b n) d")[bass.ds((u - 2) * UN, UN), :]
                                 .rearrange("(t p) d -> p t d", p=P), c_s["F"][:, :, :]).then_inc(sem["stored"], 16)
                if live(u - 1):
                    sp.wait_ge(sem["x1_aged"], due("x1_aged", u - 1))
                    sp.dma_start(x1_old[:, :, :], x1_mid[:, :, :]).then_inc(sem["x1_moved"], 16)
                if live(u):
                    if live(u - 1):
                        sp.wait_ge(sem["x1_moved"], due("x1_moved", u - 1))
                    sp.wait_ge(sem["x1"], due("x1", u))
                    sp.dma_start(x1_mid[:, :, :], x_res[:, :, :]).then_inc(sem["x1_aged"], 16)
                if live(u + 1) and live(u):
                    sp.wait_ge(sem["x1_aged"], due("x1_aged", u))
                    sp.wait_ge(sem["z1"], due("z1", u))
                    sp.dma_start(x_res[:, :, :], x_rows(u + 1)).then_inc(sem["xres_in"], 16)
                if live(i - 1):
                    if live(i - 2):
                        sp.wait_ge(sem["eaF"], due("eaF", i - 2))
                    sp.dma_start(adjs["F"][:, :, :], adj_rows(i - 1)).then_inc(sem["adjF_in"], 16)
                if live(i):
                    if live(i - 1):
                        sp.wait_ge(sem["eaE"], due("eaE", i - 1))
                    sp.dma_start(adjs["E"][:, :, :], adj_rows(i)).then_inc(sem["adjE_in"], 16)
                if live(i + 1) and live(i):
                    sp.wait_ge(sem["madd"], due("madd", i))
                    load_adj0(i + 1)
                if live(i + 2):
                    sp.wait_ge(filled["TA"], nth("TA", i + 1, 1))
                    sp.dma_start(x_ln[:, :, :], x_rows(i + 2)).then_inc(sem["x_in"], 16)

            iterations(sp, body)
            sp.wait_ge(sem["stored"], due("stored", U - 1))

        @block.tensor
        def _(pe):
            def transposes(i, g, stage_, src, u):
                for b, chunks in enumerate(((0, 1), (2,))):
                    wait_bank(pe, i, g, b)
                    for c in chunks:
                        for t in range(T):
                            col = (c - chunks[0]) * UN + t * P
                            last = nc.tensor.transpose(ps(g, b)[:, col:col + P], src[:, t, c * P:(c + 1) * P], ident[:, :])
                    last.then_inc(filled[g], 1)

            def project(out_ap, w, m, h_, node0, nodes):
                n = 0
                for c in range(C):
                    for wh, hh in ((w_lo, 0), (w_hi, 1), (w_hi, 0)):
                        last = nc.tensor.matmul(out_ap, wh[:, w, c, m * P:(m + 1) * P], h_[:, c, hh, node0:node0 + nodes],
                                                start=(n == 0), stop=(n == 3 * C - 1))
                        n += 1
                return last

            def dense(out_ap, w, h_, t):
                n = 0
                for c in range(C):
                    for hh, wh in ((1, w_hi), (0, w_lo), (0, w_hi)):
                        last = nc.tensor.matmul(out_ap, h_[:, c, hh, t * P:(t + 1) * P], wh[:, w, c, :],
                                                start=(n == 0), stop=(n == 3 * C - 1))
                        n += 1
                return last

            def similarity(i, g, stage_):
                wait_bank(pe, i, g, 0)
                h_ = hT[stage_]
                for t in range(T):
                    tile = slice(t * P, (t + 1) * P)
                    both = ps(g, 0)[:, t * 2 * P:(t + 1) * 2 * P]
                    cross = ps(g, 0)[:, t * 2 * P + P:(t + 1) * 2 * P]
                    for c in range(C):
                        nc.tensor.matmul(both, h_[:, c, 0, tile], h_[:, c, :, tile], start=(c == 0), stop=False)
                        last = nc.tensor.matmul(cross, h_[:, c, 1, tile], h_[:, c, 0, tile], start=False, stop=(c == C - 1))
                last.then_inc(filled[g], 1)

            def weigh(i, g, stage_, r, t):
                for which in range(3):
                    wait_bank(pe, i, g, 3 * t + which)
                    dense(ps(g, 3 * t + which)[:, 0:D], wround(r, which), hT[stage_], t)\
                        .then_inc(filled[g], 1)

            def flip_attention(i, g, stage_, u):
                wait_bank(pe, i, g, 0)
                pe.wait_ge(sem["attn" + stage_], due("attn" + stage_, u))
                for t in range(T):
                    last = nc.tensor.transpose(ps(g, 0)[:, t * P:(t + 1) * P],
                                               attn[stage_][:, t, :, :].rearrange("p g j -> p (g j)"), ident[:, :])
                last.then_inc(filled[g], 1)

            def context(i, g, stage_, u):
                pe.wait_ge(sem["masked" + stage_], due("masked" + stage_, u))
                for t in range(T):
                    wait_bank(pe, i, g, t)
                    pe.wait_ge(sem["d_lo" + stage_], due("d_lo" + stage_, u, 2 * (t + 1)))
                    pe.wait_ge(sem["d_hi" + stage_], due("d_hi" + stage_, u, 2 * (t + 1)))
                    n = 0
                    for side in range(2):
                        for ah, dh in ((1, 0), (0, 1), (0, 0)):
                            last = nc.tensor.matmul(ps(g, t)[:, 0:D], a_masked[:, side, ah, t, :], d_half[:, t, side, dh, :],
                                                    start=(n == 0), stop=(n == 5))
                            n += 1
                    last.then_inc(filled[g], 1)

            pe.wait_ge(pool_const, 4)

            def scores(i, u):
                pe.wait_ge(sem["qx_moved"], due("qx_moved", u))
                pe.wait_ge(sem["q_lo"], due("q_lo", u))
                for t in range(T):
                    for b in range(2):
                        wait_bank(pe, i, "S", 2 * t + b)
                        for pp in range(BP):
                            pair = BP * b + pp
                            c, slot = pair // 2, 2 * (pair % 2)
                            for g in range(G):
                                graph = G * t + g
                                dst = ps("S", 2 * t + b)[:, (pp * G + g) * N:(pp * G + g + 1) * N]
                                for n, (qh, kh) in enumerate(((1, 0), (0, 1), (0, 0))):
                                    last = nc.tensor.matmul(
                                        dst, qx[qh][:, c * UG + graph, slot:slot + 2, :].rearrange("p h q -> p (h q)"),
                                        k_half[kh][:, c, graph * N:(graph + 1) * N], start=(n == 0), stop=(n == 2))
                        last.then_inc(filled["S"], 1)

            def flip_probabilities(i, u):
                for t in range(T):
                    pe.wait_ge(sem["exp0"], due("exp0", u, t + 1))
                    for b in range(2):
                        wait_bank(pe, i, "P", 2 * t + b)
                        for pp in range(BP):
                            last = nc.tensor.transpose(ps("P", 2 * t + b)[:, pp * P:(pp + 1) * P],
                                                       s[:, t, BP * b + pp, :], ident[:, :])
                        last.then_inc(filled["P"], 1)

            def attend(i, u):
                pe.wait_ge(sem["v_lo"], due("v_lo", u))
                for t in range(T):
                    wait_bank(pe, i, "O", t)
                    pe.wait_ge(sem["p_lo"], due("p_lo", u, 4 * (t + 1)))
                    for h in range(H):
                        for n, (ph, vh) in enumerate(((1, 0), (0, 1), (0, 0))):
                            last = nc.tensor.matmul(ps("O", t)[:, h * VC:(h + 1) * VC],
                                                    px[ph][:, t, h, :, :].rearrange("p g q -> p (g q)"),
                                                    v_half[vh][:, t, h, :], start=(n == 0), stop=(n == 2))
                    last.then_inc(filled["O"], 1)

            def body(i):
                u0, uE, uF = i, i - 1, i - 2
                if live(u0):
                    if is_first(u0):
                        pe.wait_ge(w_lo_done, 3 * C)
                    pe.wait_ge(sem["tA_lo"], due("tA_lo", u0))
                    for b in range(3):
                        wait_bank(pe, i, "QK", b)
                        for part in range(2):
                            m = 2 * b + part
                            last = project(ps("QK", b)[:, part * UN:(part + 1) * UN], (WQ, WK)[m // C], m % C,
                                           hT["A"], 0, UN)
                        last.then_inc(filled["QK"], 1)
                if live(uE):
                    pe.wait_ge(sem["z1"], due("z1", uE))
                    transposes(i, "TE", "E", z1, uE)
                if live(uF):
                    pe.wait_ge(sem["zE"], due("zE", uF))
                    transposes(i, "TF", "F", c_s["E"], uF)
                if live(u0):
                    for t in range(T):
                        wait_bank(pe, i, "V", t)
                        dense(ps("V", t)[:, 0:D], WV, hT["A"], t).then_inc(filled["V"], 1)
                if live(uE):
                    pe.wait_ge(sem["tE_lo"], due("tE_lo", uE))
                    similarity(i, "UE", "E")
                if live(uF):
                    pe.wait_ge(sem["tF_lo"], due("tF_lo", uF))
                    pe.wait_ge(sem["tF_hi"], due("tF_hi", uF))
                    similarity(i, "UF", "F")
                if live(u0):
                    scores(i, u0)
                if live(uF):
                    if is_first(uF):
                        pe.wait_ge(w_lo_done, 9 * C)
                    weigh(i, "DF", "F", 1, 0)
                    flip_attention(i, "AF", "F", uF)
                    weigh(i, "DF", "F", 1, 1)
                if live(u0):
                    flip_probabilities(i, u0)
                if live(i + 1):
                    pe.wait_ge(sem["z0"], due("z0", i + 1))
                    transposes(i, "TA", "A", x_ln, i + 1)
                if live(uE):
                    if is_first(uE):
                        pe.wait_ge(w_lo_done, 6 * C)
                    weigh(i, "DE", "E", 0, 0)
                if live(uF):
                    context(i, "CF", "F", uF)
                if live(uE):
                    flip_attention(i, "AE", "E", uE)
                    weigh(i, "DE", "E", 0, 1)
                if live(u0):
                    attend(i, u0)
                if live(uE):
                    context(i, "CE", "E", uE)

            iterations(pe, body)

        @block.scalar
        def _(act):
            def split_weights(which):
                for n in which:
                    act.wait_ge(w_in[n], 16 * C)
                    for c in range(C):
                        nc.scalar.copy(w_hi[:, n, c, :], w_landing[n][c]).then_inc(w_hi_done, 1)

            split_weights(range(2))

            def norm_apply(which, u, dst, src, name):
                act.wait_ge(sem["shift" + which], due("shift" + which, u))
                act.wait_ge(sem["rstd" + which], due("rstd" + which, u))
                for t in range(T):
                    nc.scalar.activation(dst[:, t, :], src[:, t, :], ACT.Identity, bias=shift[which][:, t:t + 1],
                                         scale=rstd[which][:, t:t + 1]).then_inc(sem[name], 1)

            def relu_hi(g, stage_, u, hi_name):
                for b, chunks in enumerate(((0, 1), (2,))):
                    act.wait_ge(filled[g], nth(g, u, b))
                    nc.scalar.activation(hT[stage_][:, chunks[0]:chunks[-1] + 1, 0, :],
                                         ps(g, b)[:, 0:len(chunks) * UN].rearrange("p (c n) -> p c n", n=UN),
                                         ACT.Relu).then_inc(sem[hi_name], 1)

            def weigh_hi(stage_, u, t):
                if stage_ == "E" and live(u - 1):
                    act.wait_ge(filled["CF"], nth("CF", u - 1, t))
                for side in range(2):
                    act.wait_ge(sem["d_full" + stage_], due("d_full" + stage_, u, 2 * t + side + 1))
                    nc.scalar.copy(d_half[:, t, side, 0, :], d_full[:, side, :])\
                        .then_inc(sem["d_hi" + stage_], 1)

            def similarity_hi(g, stage_, u):
                act.wait_ge(filled[g], nth(g, u, 0))
                v = ps(g, 0)[:, :].rearrange("p (t x j) -> p t x j", t=T, x=2)
                for gr in range(G):
                    own = slice(gr * N, (gr + 1) * N)
                    nc.scalar.copy(u_s[stage_][own, :, :], v[own, :, 0, own]).then_inc(sem["u_hh" + stage_], 1)

            def similarity_exp(stage_, u):
                act.wait_ge(sem["u_sub" + stage_], due("u_sub" + stage_, u))
                nc.scalar.activation(u_s[stage_][:, :, :], u_s[stage_][:, :, :], ACT.Exp, scale=float(D) ** -0.5)\
                    .then_inc(sem["exp" + stage_], 1)

            def flip_hi(g, stage_, u):
                act.wait_ge(filled[g], nth(g, u, 0))
                nc.scalar.copy(a_half[:, 0, :, :], ps(g, 0)[:, 0:T * P].rearrange("p (t i) -> p t i", t=T))\
                    .then_inc(sem["a_hi" + stage_], 1)

            def exp_scores(u, t):
                act.wait_ge(sem["s_sub"], due("s_sub", u, t + 1))
                nc.scalar.activation(s[:, t, :, :], s[:, t, :, :], ACT.Exp).then_inc(sem["exp0"], 1)

            def query_key_hi(u, b):
                act.wait_ge(filled["QK"], nth("QK", u, b))
                for part in range(2):
                    m = 2 * b + part
                    dst = (q_half, k_half)[m // C][0]
                    nc.scalar.activation(dst[:, m % C, :], ps("QK", b)[:, part * UN:(part + 1) * UN], ACT.Identity,
                                         bias=param_cols[:, m // C, m % C:m % C + 1]).then_inc(sem["q_hi"], 1)

            def body(i):
                u0, uE, uF = i, i - 1, i - 2
                if live(u0):
                    query_key_hi(u0, 0)
                if live(uE):
                    norm_apply("1", uE, z1, x_res, "z1")
                if live(u0):
                    query_key_hi(u0, 1)
                if live(uF):
                    norm_apply("E", uF, c_s["E"], c_s["E"], "zE")
                if live(u0):
                    query_key_hi(u0, 2)
                if live(uE):
                    relu_hi("TE", "E", uE, "tE_hi")
                if live(uF):
                    if live(u0 - 1):
                        act.wait_ge(sem["x1"], due("x1", u0 - 1))
                    if live(u0):
                        act.wait_ge(sem["tA_lo"], due("tA_lo", u0))
                    for c in range(C):
                        if c != 1:
                            act.wait_ge(filled["TF"], nth("TF", uF, c // 2))
                        src = ps("TF", c // 2)[:, (c % 2) * UN:(c % 2 + 1) * UN]
                        scale, shift = param_cols[:, 2, c:c + 1], param_cols[:, 3, c:c + 1]
                        nc.scalar.activation(hT_full[:, c, :], src, ACT.Relu, bias=shift, scale=scale)\
                            .then_inc(sem["tF_full"], 1)
                        nc.scalar.activation(hT["F"][:, c, 0, :], src, ACT.Relu, bias=shift, scale=scale)\
                            .then_inc(sem["tF_hi"], 1)
                if live(u0):
                    for t in range(T):
                        act.wait_ge(filled["V"], nth("V", u0, t))
                        nc.scalar.copy(v_half[0][:, t, :, 0:HD], ps("V", t)[:, 0:D].rearrange("p (h d) -> p h d", h=H))\
                            .then_inc(sem["v_hi"], 1)
                if is_first(u0):
                    split_weights(range(6, 9))
                if live(uE):
                    similarity_hi("UE", "E", uE)
                if live(uF):
                    similarity_hi("UF", "F", uF)
                if live(uE):
                    similarity_exp("E", uE)
                if live(uF):
                    similarity_exp("F", uF)
                if live(u0):
                    exp_scores(u0, 0)
                    exp_scores(u0, 1)
                if live(uF):
                    flip_hi("AF", "F", uF)
                    weigh_hi("F", uF, 0)
                if live(i + 1):
                    norm_apply("0", i + 1, x_ln, x_ln, "z0")
                if is_first(i + 1):
                    split_weights(range(2, 3))
                if live(uF):
                    weigh_hi("F", uF, 1)
                if live(u0):
                    for n in range(2 * T):
                        act.wait_ge(filled["P"], nth("P", u0, n))
                        t, b = n // 2, n % 2
                        for g in range(G):
                            own = slice(g * N, (g + 1) * N)
                            nc.scalar.copy(px[0][own, t, 2 * BP * b:2 * BP * (b + 1), g, :],
                                           ps("P", n)[own, 0:BP * P].rearrange("p (h q) -> p h q", q=N))\
                                .then_inc(sem["p_hi"], 1)
                if live(i + 1):
                    for b, chunks in enumerate(((0, 1), (2,))):
                        act.wait_ge(filled["TA"], nth("TA", i + 1, b))
                        src = ps("TA", b)[:, 0:len(chunks) * UN].rearrange("p (c n) -> p c n", n=UN)
                        span = slice(chunks[0], chunks[-1] + 1)
                        nc.scalar.activation(hT_full[:, span, :], src, ACT.Relu).then_inc(sem["tA_full"], 1)
                        nc.scalar.activation(hT["A"][:, span, 0, :], src, ACT.Relu).then_inc(sem["tA_hi"], 1)
                if is_first(i + 1):
                    split_weights(range(3, 6))
                    act.wait_ge(const_in, 48)
                if live(uE):
                    weigh_hi("E", uE, 0)
                    flip_hi("AE", "E", uE)
                    weigh_hi("E", uE, 1)

            iterations(act, body)

        @block.gpsimd
        def _(pool):
            nc.gpsimd.memset(ident[:, :], 0.0)
            nc.gpsimd.memset(later[:, :], 0.0)
            nc.gpsimd.memset(half_power[:, :], -0.5)
            nc.gpsimd.memset(earlier[:, :], 0.0).then_inc(pool_const, 1)
            pool.wait_ge(pool_const, 1)
            for g in range(G):
                own = slice(g * N, (g + 1) * N)
                nc.gpsimd.memset(later[own, own], 1.0)
                last = nc.gpsimd.memset(earlier[own, own], 1.0)
            last.then_inc(pool_const, 1)
            pool.wait_ge(pool_const, 2)
            nc.gpsimd.affine_select(out=ident[:, :], in_=ident[:, :], compare_op=ALU.not_equal, fill=1.0,
                                    base=0, pattern=[[-1, P]], channel_multiplier=1)
            nc.gpsimd.affine_select(out=later[:, :], in_=later[:, :], compare_op=ALU.is_gt, fill=0.0,
                                    base=0, pattern=[[-1, P]], channel_multiplier=1)
            nc.gpsimd.affine_select(out=earlier[:, :], in_=earlier[:, :], compare_op=ALU.is_gt, fill=0.0,
                                    base=0, pattern=[[1, P]], channel_multiplier=-1).then_inc(pool_const, 2)

            def zero_fill():
                pool.wait_ge(w_lo_done, 3 * C)
                for half in range(2):
                    nc.gpsimd.memset(qx[half].rearrange("p a b c -> p (a b c)").bitcast(F32), 0.0)
                for half in range(2):
                    last = nc.gpsimd.memset(px[half][:, :, :, :, :].rearrange("p t h g q -> p (t h g q)").bitcast(F32),
                                            0.0)
                last.then_inc(zeroed, 1)

            def inverse_root(which, u):
                pool.wait_ge(sem["ve" + which], due("ve" + which, u))
                nc.gpsimd.tensor_tensor(rstd[which][:, :], ve[which][:, :], half_power[:, :], ALU.pow)\
                    .then_inc(sem["rstd" + which], 1)
                if which != "F":
                    pool.wait_ge(sem["neg_mean" + which], due("neg_mean" + which, u))
                    pool.wait_ge(sem["rstd" + which], due("rstd" + which, u))
                    nc.gpsimd.tensor_tensor(shift[which][:, :], neg_mean[which][:, :], rstd[which][:, :], ALU.mult)\
                        .then_inc(sem["shift" + which], 1)

            def weigh_adjacency(stage_, u):
                pool.wait_ge(sem["adj" + stage_ + "_in"], due("adj" + stage_ + "_in", u))
                pool.wait_ge(sem["exp" + stage_], due("exp" + stage_, u))
                nc.gpsimd.tensor_tensor(ea[stage_][:, :, :], u_s[stage_][:, :, :], adjs[stage_][:, :, :], ALU.mult)\
                    .then_inc(sem["ea" + stage_], 1)

            def weigh_lo(stage_, u, t):
                for side in range(2):
                    pool.wait_ge(sem["d_hi" + stage_], due("d_hi" + stage_, u, 2 * t + side + 1))
                    nc.gpsimd.tensor_tensor(d_half[:, t, side, 1, :], d_full[:, side, :],
                                            d_half[:, t, side, 0, :].bitcast(F32), ALU.subtract)\
                        .then_inc(sem["d_lo" + stage_], 1)

            def subtract_max(u, t):
                pool.wait_ge(sem["s_max"], due("s_max", u, t + 1))
                rows_of = s[:, t, :, :].rearrange("p a (g k) -> p (a g) k", k=N)
                nc.gpsimd.tensor_tensor(rows_of, rows_of, s_max[:, t, :].unsqueeze(2).to_broadcast([P, PAIRS * G, N]),
                                        ALU.subtract).then_inc(sem["s_sub"], 1)

            def mask(stage_, u):
                pool.wait_ge(sem["a_lo" + stage_], due("a_lo" + stage_, u))
                pool.wait_ge(sem["a_hi" + stage_], due("a_hi" + stage_, u))
                src = a_half[:, :, :, :].rearrange("p x t i -> p (x t) i").bitcast(F32)
                for side, m in enumerate((later, earlier)):
                    nc.gpsimd.tensor_tensor(a_masked[:, side, :, :, :].rearrange("p x t i -> p (x t) i"), src,
                                            m[:, :].unsqueeze(1).to_broadcast([P, 2 * T, P]), ALU.mult)\
                        .then_inc(sem["masked" + stage_], 1)

            def body(i):
                u0, uE, uF = i, i - 1, i - 2
                if live(uF):
                    for c in range(C):
                        pool.wait_ge(sem["tF_hi"], due("tF_hi", uF, c + 1))
                        pool.wait_ge(sem["tF_full"], due("tF_full", uF, c + 1))
                        nc.gpsimd.tensor_tensor(hT["F"][:, c, 1, :], hT_full[:, c, :],
                                                hT["F"][:, c, 0, :].bitcast(F32), ALU.subtract).then_inc(sem["tF_lo"], 1)
                if live(uE):
                    weigh_adjacency("E", uE)
                if live(uF):
                    weigh_adjacency("F", uF)
                if live(u0):
                    subtract_max(u0, 0)
                    subtract_max(u0, 1)
                if live(i + 1):
                    inverse_root("0", i + 1)
                if live(uF):
                    weigh_lo("F", uF, 0)
                    mask("F", uF)
                    weigh_lo("F", uF, 1)
                if live(u0):
                    pool.wait_ge(sem["xres_in"], due("xres_in", u0))
                    nc.gpsimd.tensor_tensor(x_res[:, :, :], x_res[:, :, :],
                                            param_rows[:, 0:1, :].to_broadcast([P, T, D]), ALU.add)\
                        .then_inc(sem["xb"], 1)
                if live(i + 1):
                    for b, span in enumerate((slice(0, 2), slice(2, 3))):
                        pool.wait_ge(sem["tA_hi"], due("tA_hi", i + 1, b + 1))
                        pool.wait_ge(sem["tA_full"], due("tA_full", i + 1, b + 1))
                        nc.gpsimd.tensor_tensor(hT["A"][:, span, 1, :], hT_full[:, span, :],
                                                hT["A"][:, span, 0, :].bitcast(F32), ALU.subtract)\
                            .then_inc(sem["tA_lo"], 1)
                if is_first(i + 1):
                    zero_fill()
                    pool.wait_ge(const_in, 48)
                if live(uE):
                    weigh_lo("E", uE, 0)
                    mask("E", uE)
                    weigh_lo("E", uE, 1)
                if live(u0):
                    pool.wait_ge(sem["xb"], due("xb", u0))
                    for t in range(T):
                        pool.wait_ge(sem["o_ready"], due("o_ready", u0, t + 1))
                        nc.gpsimd.tensor_tensor(x_res[:, t, :], o[:, t, :], x_res[:, t, :], ALU.add)\
                            .then_inc(sem["x1"], 1)
                    inverse_root("1", u0)
                if live(uE):
                    inverse_root("E", uE)
                if live(uF):
                    inverse_root("F", uF)

            iterations(pool, body)

        @block.vector
        def _(dve):
            def split_weights(which):
                for n in which:
                    for c in range(C):
                        dve.wait_ge(w_hi_done, C * n + c + 1)
                        nc.vector.tensor_tensor(w_lo[:, n, c, :], w_landing[n][c], w_hi[:, n, c, :].bitcast(F32),
                                                ALU.subtract).then_inc(w_lo_done, 1)

            for half in range(2):
                nc.vector.memset(v_half[half][:, :, :, HD:VC], 1.0 - half)
            dve.wait_ge(pool_const, 4)
            nc.vector.tensor_tensor(eye[:, :], ident[:, 0:N], ident[:, N:P], ALU.add).then_inc(dve_const, 1)
            dve.wait_ge(dve_const, 1)

            def norm_stats(which, u, src, source_ready):
                eps = LN_EPS["01EF".index(which)]
                for t in range(T):
                    dve.wait_ge(sem[source_ready], due(source_ready, u, t + 1 if COUNTS[source_ready] == T else None))
                    nc.vector.bn_stats(stats[which][:, t, :], src[:, t, :]).then_inc(sem["stats" + which], 1)
                dve.wait_ge(sem["stats" + which], due("stats" + which, u))
                nc.vector.memset(ve[which][:, :], eps)
                for t in range(T):
                    nc.vector.bn_aggr(mv[which][:, t, :], stats[which][:, t, :]).then_inc(sem["mv" + which], 1)
                dve.wait_ge(sem["mv" + which], due("mv" + which, u))
                nc.vector.tensor_tensor(ve[which][:, :], ve[which][:, :], mv[which][:, :, 1], ALU.add)\
                    .then_inc(sem["ve" + which], 1)
                if which != "F":
                    nc.vector.tensor_scalar(neg_mean[which][:, :], mv[which][:, :, 0], -1.0, None, ALU.mult)\
                        .then_inc(sem["neg_mean" + which], 1)

            def relu_lo(g, stage_, u, hi_name, lo_name):
                for b, chunks in enumerate(((0, 1), (2,))):
                    dve.wait_ge(sem[hi_name], due(hi_name, u, b + 1))
                    span = slice(chunks[0], chunks[-1] + 1)
                    nc.vector.scalar_tensor_tensor(hT[stage_][:, span, 1, :],
                                                   ps(g, b)[:, 0:len(chunks) * UN].rearrange("p (c n) -> p c n", n=UN), 0.0,
                                                   hT[stage_][:, span, 0, :].bitcast(F32), ALU.max, ALU.subtract)\
                        .then_inc(sem[lo_name], 1)

            def similarity_softmax_1(g, stage_, u):
                dve.wait_ge(sem["u_hh" + stage_], due("u_hh" + stage_, u))
                v = ps(g, 0)[:, :].rearrange("p (t x j) -> p t x j", t=T, x=2)
                for gr in range(G):
                    own = slice(gr * N, (gr + 1) * N)
                    nc.vector.tensor_tensor(u_s[stage_][own, :, :], v[own, :, 1, own], u_s[stage_][own, :, :], ALU.add)\
                        .then_inc(sem["u_sum" + stage_], 1)
                dve.wait_ge(sem["u_sum" + stage_], due("u_sum" + stage_, u))
                nc.vector.tensor_reduce(u_max[stage_][:, :], u_s[stage_][:, :, :], AX_X, ALU.max)\
                    .then_inc(sem["u_max" + stage_], 1)
                dve.wait_ge(sem["u_max" + stage_], due("u_max" + stage_, u))
                nc.vector.tensor_tensor(u_s[stage_][:, :, :], u_s[stage_][:, :, :],
                                        u_max[stage_][:, :].unsqueeze(2).to_broadcast([P, T, N]), ALU.subtract)\
                    .then_inc(sem["u_sub" + stage_], 1)

            def similarity_softmax_2(stage_, u):
                dve.wait_ge(sem["exp" + stage_], due("exp" + stage_, u))
                nc.vector.tensor_reduce(esum[stage_][:, :], u_s[stage_][:, :, :], AX_X, ALU.add)\
                    .then_inc(sem["esum" + stage_], 1)
                dve.wait_ge(sem["ea" + stage_], due("ea" + stage_, u))
                nc.vector.tensor_reduce(easum[stage_][:, :], ea[stage_][:, :, :], AX_X, ALU.add)\
                    .then_inc(sem["easum" + stage_], 1)
                dve.wait_ge(sem["esum" + stage_], due("esum" + stage_, u))
                dve.wait_ge(sem["easum" + stage_], due("easum" + stage_, u))
                nc.vector.scalar_tensor_tensor(den[stage_][:, :], esum[stage_][:, :], 1e-10, easum[stage_][:, :],
                                               ALU.mult, ALU.add).then_inc(sem["den" + stage_], 1)
                dve.wait_ge(sem["den" + stage_], due("den" + stage_, u))
                nc.vector.reciprocal(rden[stage_][:, :], den[stage_][:, :]).then_inc(sem["rden" + stage_], 1)
                dve.wait_ge(sem["rden" + stage_], due("rden" + stage_, u))
                nc.vector.tensor_tensor(attn[stage_][:, :, :, :],
                                        ea[stage_][:, :, :].unsqueeze(2).to_broadcast([P, T, G, N]),
                                        rden[stage_][:, :].unsqueeze(2).unsqueeze(3).to_broadcast([P, T, G, N]), ALU.mult)\
                    .then_inc(sem["attn" + stage_], 1)

            def diagonal(stage_, u):
                dve.wait_ge(sem["attn" + stage_], due("attn" + stage_, u))
                nc.vector.tensor_tensor(u_s[stage_][:, :, :], attn[stage_][:, :, 0, :],
                                        eye[:, :].unsqueeze(1).to_broadcast([P, T, N]), ALU.mult)\
                    .then_inc(sem["de" + stage_], 1)
                dve.wait_ge(sem["de" + stage_], due("de" + stage_, u))
                nc.vector.tensor_reduce(diag[stage_][:, :], u_s[stage_][:, :, :], AX_X, ALU.add)\
                    .then_inc(sem["diag" + stage_], 1)

            def weigh_full(g, stage_, r, u, t):
                for which in range(3):
                    dve.wait_ge(filled[g], nth(g, u, 3 * t + which))
                    if which == 1:
                        if stage_ == "F" and live(u - 1):
                            dve.wait_ge(sem["stored"], due("stored", u - 1))
                        dst, name = c_s[stage_][:, t, :], "hs"
                    else:
                        if t == 1:
                            dve.wait_ge(sem["d_lo" + stage_], due("d_lo" + stage_, u, which // 2 + 1))
                        elif stage_ == "E" and live(u - 1):
                            dve.wait_ge(sem["d_loF"], due("d_loF", u - 1, 3 + which // 2))
                        elif stage_ == "F":
                            dve.wait_ge(sem["d_loE"], due("d_loE", u, 3 + which // 2))
                        dst, name = d_full[:, which // 2, :], "d_full"
                    nc.vector.tensor_tensor(dst, ps(g, 3 * t + which)[:, 0:D], bias_rows[:, 3 * r + which, :], ALU.add)\
                        .then_inc(sem[name + stage_], 1)

            def flip_lo(g, stage_, u):
                dve.wait_ge(sem["a_hi" + stage_], due("a_hi" + stage_, u))
                nc.vector.tensor_tensor(a_half[:, 1, :, :], ps(g, 0)[:, 0:T * P].rearrange("p (t i) -> p t i", t=T),
                                        a_half[:, 0, :, :].bitcast(F32), ALU.subtract).then_inc(sem["a_lo" + stage_], 1)

            def add_same(g, stage_, u):
                dve.wait_ge(sem["diag" + stage_], due("diag" + stage_, u))
                dve.wait_ge(sem["hs" + stage_], due("hs" + stage_, u))
                for t in range(T):
                    dve.wait_ge(filled[g], nth(g, u, t))
                    nc.vector.scalar_tensor_tensor(c_s[stage_][:, t, :], c_s[stage_][:, t, :], diag[stage_][:, t:t + 1],
                                                   ps(g, t)[:, 0:D], ALU.mult, ALU.add)\
                        .then_inc(sem["c_ready" + stage_], 1)

            def score_sums(u, t):
                for b in range(2):
                    dve.wait_ge(filled["S"], nth("S", u, 2 * t + b))
                    nc.vector.scalar_tensor_tensor(
                        s[:, t, BP * b:BP * (b + 1), :],
                        ps("S", 2 * t + b)[:, 0:BP * P].rearrange("p (a k) -> p a k", a=BP), float(HD) ** -0.5,
                        madd[:, G * t:G * (t + 1), :].rearrange("p g k -> p (g k)").unsqueeze(1)
                        .to_broadcast([P, BP, P]), ALU.mult, ALU.add).then_inc(sem["s_sum"], 1)
                dve.wait_ge(sem["s_sum"], due("s_sum", u, 2 * (t + 1)))
                nc.vector.tensor_reduce(s_max[:, t, :], s[:, t, :, :].rearrange("p a (g k) -> p (a g) k", k=N),
                                        AX_X, ALU.max).then_inc(sem["s_max"], 1)

            def query_key_lo(u, b):
                dve.wait_ge(sem["q_hi"], due("q_hi", u, 2 * b + 2))
                for part in range(2):
                    m = 2 * b + part
                    half = (q_half, k_half)[m // C]
                    nc.vector.scalar_tensor_tensor(half[1][:, m % C, :], ps("QK", b)[:, part * UN:(part + 1) * UN],
                                                   param_cols[:, m // C, m % C:m % C + 1], half[0][:, m % C, :],
                                                   ALU.add, ALU.subtract).then_inc(sem["q_lo"], 1)

            def body(i):
                u0, uE, uF, uO = i, i - 1, i - 2, i - 3
                if live(u0):
                    query_key_lo(u0, 0)
                    query_key_lo(u0, 1)
                if live(uO):
                    dve.wait_ge(sem["rstdF"], due("rstdF", uO))
                    for t in range(T):
                        nc.vector.scalar_tensor_tensor(c_s["F"][:, t, :], c_s["F"][:, t, :], mv["F"][:, t, 0:1],
                                                       param_rows[:, 1, :], ALU.subtract, ALU.mult)\
                            .then_inc(sem["yg"], 1)
                    for t in range(T):
                        dve.wait_ge(sem["yg"], due("yg", uO, t + 1))
                        nc.vector.scalar_tensor_tensor(c_s["F"][:, t, :], c_s["F"][:, t, :], rstd["F"][:, t:t + 1],
                                                       param_rows[:, 2, :], ALU.mult, ALU.add)\
                            .then_inc(sem["yb"], 1)
                if live(u0):
                    query_key_lo(u0, 2)
                if live(uE):
                    relu_lo("TE", "E", uE, "tE_hi", "tE_lo")
                if live(uO):
                    dve.wait_ge(sem["x1_moved"], due("x1_moved", uO))
                    for t in range(T):
                        dve.wait_ge(sem["yb"], due("yb", uO, t + 1))
                        nc.vector.scalar_tensor_tensor(c_s["F"][:, t, :], c_s["F"][:, t, :], 0.0, x1_old[:, t, :],
                                                       ALU.max, ALU.add).then_inc(sem["out_ready"], 1)
                if live(u0):
                    dve.wait_ge(sem["adj0_in"], due("adj0_in", u0))
                    nc.vector.tensor_scalar(madd[:, :, :], adj0[:, :, :], 0.0, MASKED, ALU.is_le, ALU.mult)\
                        .then_inc(sem["s_t"], 1)
                    for t in range(T):
                        dve.wait_ge(sem["v_hi"], due("v_hi", u0, t + 1))
                        nc.vector.tensor_tensor(v_half[1][:, t, :, 0:HD], ps("V", t)[:, 0:D].rearrange("p (h d) -> p h d", h=H),
                                                v_half[0][:, t, :, 0:HD], ALU.subtract).then_inc(sem["v_lo"], 1)
                    dve.wait_ge(sem["s_t"], due("s_t", u0))
                    nc.vector.scalar_tensor_tensor(madd[:, :, :], adj0[:, :, :], beta_col[:, 0:1], madd[:, :, :],
                                                   ALU.mult, ALU.add).then_inc(sem["madd"], 1)
                if live(uE):
                    similarity_softmax_1("UE", "E", uE)
                if live(uF):
                    similarity_softmax_1("UF", "F", uF)
                if live(u0):
                    dve.wait_ge(sem["madd"], due("madd", u0))
                    score_sums(u0, 0)
                if live(uF):
                    similarity_softmax_2("F", uF)
                if live(u0):
                    score_sums(u0, 1)
                if live(i + 1):
                    norm_stats("0", i + 1, x_ln, "x_in")
                    if is_first(i + 1):
                        split_weights(range(6))
                        dve.wait_ge(const_in, 48)
                if is_first(u0):
                    split_weights(range(6, 9))
                if is_first(uE):
                    dve.wait_ge(bias_in, 16)
                if live(uF):
                    weigh_full("DF", "F", 1, uF, 0)
                    flip_lo("AF", "F", uF)
                if live(uE):
                    similarity_softmax_2("E", uE)
                if live(uF):
                    weigh_full("DF", "F", 1, uF, 1)
                    diagonal("F", uF)
                if live(uE):
                    diagonal("E", uE)
                if live(u0):
                    for n in range(2 * T):
                        t, b = n // 2, n % 2
                        dve.wait_ge(sem["p_hi"], due("p_hi", u0, 2 * n + 2))
                        for g in range(G):
                            own = slice(g * N, (g + 1) * N)
                            at = (own, t, slice(2 * BP * b, 2 * BP * (b + 1)), g)
                            nc.vector.tensor_tensor(px[1][at], ps("P", n)[own, 0:BP * P].rearrange("p (h q) -> p h q", q=N),
                                                    px[0][at], ALU.subtract).then_inc(sem["p_lo"], 1)
                if live(uE):
                    weigh_full("DE", "E", 0, uE, 0)
                if live(uF):
                    add_same("CF", "F", uF)
                if live(uE):
                    flip_lo("AE", "E", uE)
                if live(uF):
                    norm_stats("F", uF, c_s["F"], "c_readyF")
                if live(uE):
                    weigh_full("DE", "E", 0, uE, 1)
                if live(u0):
                    if live(uF):
                        dve.wait_ge(sem["tF_lo"], due("tF_lo", uF))
                    if live(i + 1):
                        dve.wait_ge(sem["tA_lo"], due("tA_lo", i + 1))
                    for t in range(T):
                        dve.wait_ge(filled["O"], nth("O", u0, t))
                        v = ps("O", t)[:, 0:H * VC].rearrange("p (h c) -> p h c", c=VC)
                        nc.vector.reciprocal(o_rsum[:, t, :], v[:, :, HD]).then_inc(sem["osum"], 1)
                        dve.wait_ge(sem["osum"], due("osum", u0, t + 1))
                        nc.vector.tensor_tensor(o[:, t, :].rearrange("p (h d) -> p h d", h=H), v[:, :, 0:HD],
                                                o_rsum[:, t, :].unsqueeze(2).to_broadcast([P, H, HD]), ALU.mult)\
                            .then_inc(sem["o_ready"], 1)
                if live(uE):
                    add_same("CE", "E", uE)
                if live(u0):
                    norm_stats("1", u0, x_res, "x1")
                if live(uE):
                    norm_stats("E", uE, c_s["E"], "c_readyE")

            iterations(dve, body)


def kernel(x, adj, L0_gnn_Wq, L0_gnn_bq, L0_gnn_Wk, L0_gnn_bk, L0_gnn_Wv, L0_gnn_bv, L0_gnn_beta, L1_gnn_Wl, L1_gnn_bl,
           L1_gnn_Ws, L1_gnn_bs, L1_gnn_Wr, L1_gnn_br, L1_gnn_ln_w, L1_gnn_ln_b):
    import numpy as np
    import concourse.bacc as bacc
    from concourse.bass_utils import run_bass_kernel_spmd

    rounds = [np.asarray(w)[r].T for r in range(2) for w in (L1_gnn_Wl, L1_gnn_Ws, L1_gnn_Wr)]
    by_feature = [L0_gnn_bq, L0_gnn_bk, L1_gnn_ln_w[0], L1_gnn_ln_b[0]]
    arrays = {
        "x": np.asarray(x), "adj": np.asarray(adj),
        "weights": np.stack([np.asarray(w) for w in (L0_gnn_Wq, L0_gnn_Wk, L0_gnn_Wv)] + rounds),
        "cols": np.stack([np.asarray(b) for b in by_feature]).reshape(4, C, P).transpose(2, 0, 1),
        "rows": np.concatenate([np.asarray(b) for b in (L0_gnn_bv, L1_gnn_ln_w[1], L1_gnn_ln_b[1])]),
        "biases": np.concatenate([np.asarray(b)[r] for r in range(2) for b in (L1_gnn_bl, L1_gnn_bs, L1_gnn_br)])
                    .reshape(6, D),
        "beta": np.asarray(L0_gnn_beta).reshape(1),
    }
    arrays = {n: np.ascontiguousarray(a) for n, a in arrays.items()}
    nc = bacc.Bacc("TRN2", target_bir_lowering=False, num_devices=1)
    args = [nc.dram_tensor(n, a.shape, mybir.dt.from_np(a.dtype), kind="ExternalInput").ap() for n, a in arrays.items()]
    out = nc.dram_tensor("out", arrays["x"].shape, F32, kind="ExternalOutput").ap()
    build(nc, *args, out)
    return run_bass_kernel_spmd(nc, [arrays], core_ids=[0]).results[0]["out"]
```
